# Optimizing a Trainium2 kernel written in Bass

```python
import numpy as np
import jax
import jax.numpy as jnp

def _softmax(x, axis=-1):
    return jax.nn.softmax(x, axis=axis)

def _gelu(x):
    return jax.nn.gelu(x, approximate=True)

def _silu(x):
    return jax.nn.silu(x)

def _sigmoid(x):
    return jax.nn.sigmoid(x)

def _layernorm(x, axis=-1, eps=1e-05):
    m = jnp.mean(x, axis=axis, keepdims=True)
    v = jnp.var(x, axis=axis, keepdims=True)
    return (x - m) / jnp.sqrt(v + eps)

def _scatter_add(tgt, idx, src, axis=0):
    return tgt.at[idx].add(src)

def _segment_sum(src, seg, n):
    return jax.ops.segment_sum(src, seg, n)
kernel_name = 'mk_adj_resnorm_d2_adj_r2_a46466'

def setup_inputs(seed: int=0):
    np.random.seed(seed)
    _w = jnp.asarray

    def _rec_inputs():
        import jax
        import jax.numpy as jnp
        _gk = jax.random.key(seed)
        x = -0.000929 + 1 * jax.random.normal(jax.random.fold_in(_gk, 1), (8192, 128), jnp.float32)
        _w = (1.0 + jnp.arange(8192, dtype=jnp.float32)) ** (-0.5)
        _w = _w / _w.mean()
        _pij = jnp.clip(0.000244141 * _w[:, None] * _w[None, :], 0.0, 1.0)
        _a = jax.random.uniform(jax.random.fold_in(_gk, 2), (8192, 8192)) < _pij
        _a = jnp.logical_or(_a, jnp.swapaxes(_a, -1, -2))
        _a = jnp.logical_or(_a, jnp.eye(8192, dtype=bool))
        _af = _a.astype(jnp.float32)
        _af = _af * jax.random.uniform(jax.random.fold_in(_gk, 3), (8192, 8192), jnp.float32, 0.05, 0.0598829)
        adj = _af
        return (x, adj)
    x, adj = _rec_inputs()

    def _L0_gnn_setup():
        import jax, jax.numpy as jnp
        import numpy as np
        N, C_IN, C_OUT, K = (4096, 128, 128, 3)
        key = jax.random.key(seed)
        k1, k2, k3 = jax.random.split(key, 3)
        x = jax.random.normal(k1, (N, C_IN), dtype=jnp.float32)
        L = jax.random.normal(k2, (N, N), dtype=jnp.float32) / np.sqrt(N).astype(np.float32)
        W = jax.random.normal(k3, (K, C_OUT, C_IN), dtype=jnp.float32) / np.sqrt(C_IN).astype(np.float32)
        return {'x': x, 'L': L, 'W': W}
    _L0_gnn_all = _L0_gnn_setup()
    _L0_gnn_in = {k: v for k, v in _L0_gnn_all.items() if k in ('W',)}
    del _L0_gnn_all

    def _L1_gnn_setup():
        import jax, jax.numpy as jnp
        import numpy as np
        N, DIN, DOUT = (4096, 128, 128)
        NEG = -9000000000000000.0
        ALPHA = 0.2
        key = jax.random.key(seed)
        kx, ka, kw, ks, kr = jax.random.split(key, 5)
        X = jax.random.normal(kx, (N, DIN), dtype=jnp.float32)
        A = (jax.random.uniform(ka, (N, N)) < 0.01).astype(jnp.float32)
        A = A.at[jnp.arange(N), jnp.arange(N)].set(1.0)
        lim_w = float(np.sqrt(6.0 / (DIN + DOUT)))
        W = jax.random.uniform(kw, (DOUT, DIN), jnp.float32, -lim_w, lim_w)
        b = jnp.zeros((DOUT,), jnp.float32)
        lim_a = float(np.sqrt(6.0 / (DOUT + 1)))
        a_s = jax.random.uniform(ks, (DOUT, 1), jnp.float32, -lim_a, lim_a)
        a_r = jax.random.uniform(kr, (DOUT, 1), jnp.float32, -lim_a, lim_a)
        return {'X': X, 'A': A, 'W': W, 'b': b, 'a_s': a_s, 'a_r': a_r}
    _L1_gnn_all = _L1_gnn_setup()
    _L1_gnn_in = {k: v for k, v in _L1_gnn_all.items() if k in ('W', 'b', 'a_s', 'a_r')}
    del _L1_gnn_all
    return {'x': x, 'adj': adj, 'L0_gnn_W': _L0_gnn_in['W'], 'L1_gnn_W': _L1_gnn_in['W'], 'L1_gnn_b': _L1_gnn_in['b'], 'L1_gnn_a_s': _L1_gnn_in['a_s'], 'L1_gnn_a_r': _L1_gnn_in['a_r']}

def reference(x, adj, L0_gnn_W, L1_gnn_W, L1_gnn_b, L1_gnn_a_s, L1_gnn_a_r):
    import jax
    import jax.numpy as jnp

    def _L0_gnn_ref(x, L, W):
        import jax, jax.numpy as jnp
        import numpy as np
        N, C_IN, C_OUT, K = (4096, 128, 128, 3)
        k = W.shape[0]
        T0 = x
        T1 = L @ x
        out = T0 @ W[0].T
        if k > 1:
            out = out + T1 @ W[1].T
        for j in range(2, k):
            T2 = 2.0 * (L @ T1) - T0
            out = out + T2 @ W[j].T
            T0, T1 = (T1, T2)
        return out

    def _L1_gnn_ref(X, A, W, b, a_s, a_r):
        import jax, jax.numpy as jnp
        import numpy as np
        N, DIN, DOUT = (4096, 128, 128)
        NEG = -9000000000000000.0
        ALPHA = 0.2
        H = X @ W.T + b
        s = H @ a_s
        r = H @ a_r
        e = jax.nn.leaky_relu(A * s + A * r.T, negative_slope=ALPHA)
        masked = jnp.where(A > 0, e, NEG)
        att = jax.nn.softmax(masked, axis=1)
        H_out = att @ H
        return H_out
    x = _layernorm(x + _L0_gnn_ref(x, adj, L0_gnn_W), axis=-1)
    x = _layernorm(x + _L1_gnn_ref(x, adj, L1_gnn_W, L1_gnn_b, L1_gnn_a_s, L1_gnn_a_r), axis=-1)
    return x

_drawn_inputs = setup_inputs


def setup_inputs(seed=0):
    import zlib

    import numpy as np

    out = dict(_drawn_inputs(seed))
    spreads = {'L1_gnn_b': (0.0, 0.1)}
    factors = {'L1_gnn_a_s': 8.0, 'L1_gnn_a_r': 3.342}
    for name, (base, spread) in spreads.items():
        noise = np.random.default_rng([zlib.crc32(name.encode()), seed]).standard_normal(out[name].shape)
        drawn = base * np.exp(spread * noise) if base else spread * noise
        out[name] = jnp.asarray(drawn.astype(out[name].dtype))
    for name, factor in factors.items():
        out[name] = (out[name] * factor).astype(out[name].dtype)
    return out
```

```python
from contextlib import ExitStack

import numpy as np
import concourse.bass as bass
from concourse import mybir

P = 128
BANK = 512
SPAN = 2048
RING = 4
MASKED = 2.0 ** 53
LOWEST = -3.0e38
SLOPE = 0.2
EPS = 1e-5

F32 = mybir.dt.float32
F32R = mybir.dt.float32r
ALU = mybir.AluOpType
ACT = mybir.ActivationFunctionType
AX = mybir.AxisListType


def wait_alone(engine, semaphore, value):
    engine.wait_ge(semaphore, 1)
    engine.wait_ge(semaphore, value)


def diffuse(nc, name, tiles, T, nodes, mem, second):
    SUP = T * P // SPAN
    QUADS = T // RING
    BANKS = SPAN // BANK
    ring, psum = mem["ring"], mem["psum"]
    out, xT = mem["t2T" if second else "t1T"], mem["xT"]
    with ExitStack() as ctx:
        def sem(name):
            return ctx.enter_context(nc.semaphore(name))

        def sbuf(name, shape, dtype):
            return ctx.enter_context(nc.sbuf_tensor(name, shape, dtype))

        high = sbuf(name + "_high", [P, 2, SPAN], F32R)
        low = sbuf(name + "_low", [P, 2, SPAN], F32R)
        w_high = sbuf(name + "_w_high", [P, RING, P], F32R)
        w_low = sbuf(name + "_w_low", [P, RING, P], F32R)
        tile_in = [sem(f"{name}_tile_in{k}") for k in range(RING)]
        high_ready = sem(name + "_high_ready")
        low_ready = sem(name + "_low_ready")
        w_full = sbuf(name + "_w_full", [P, RING, P], F32)
        w_copied = sem(name + "_w_copied")
        w_ready = sem(name + "_w_ready")
        tile_summed = sem(name + "_tile_summed")
        bank_free = sem(name + "_bank_free")
        block = ctx.enter_context(nc.Block())
        @block.sync
        def _(sp):
            for k in range(RING):
                sp.dma_start(ring[:, k, :], tiles[k, :, :]).then_inc(tile_in[k], 16)
            with sp.Fori(1, SUP * QUADS) as q:
                for k in range(RING):
                    sp.wait_ge(low_ready, q * RING + (k - RING + 1))
                    sp.dma_start(ring[:, k, :], tiles[bass.ds(q * RING + k, 1), :, :].rearrange("a p n -> (a p) n"))\
                        .then_inc(tile_in[k], 16)

        @block.gpsimd
        def _(pool):
            def split(s, q, k, first):
                n = (s * QUADS + q) * RING + k
                if not first:
                    pool.wait_ge(tile_summed, n - (RING - 1))
                src = nodes[:, bass.ds(q * RING + k, 1), :].rearrange("p a d -> p (a d)")
                nc.gpsimd.tensor_copy(w_full[:, k, :], src).then_inc(w_copied, 1)
                nc.gpsimd.tensor_copy(w_high[:, k, :], src).then_inc(w_copied, 1)
                pool.wait_ge(w_copied, 2 * n + 2)
                nc.gpsimd.tensor_tensor(w_low[:, k, :], w_full[:, k, :], w_high[:, k, :].bitcast(F32), ALU.subtract)\
                    .then_inc(w_ready, 1)

            for k in range(RING):
                split(0, 0, k, True)
            with pool.Fori(1, QUADS) as q:
                for k in range(RING):
                    split(0, q, k, False)
            with pool.Fori(1, SUP) as s:
                with pool.Fori(0, QUADS) as q:
                    for k in range(RING):
                        split(s, q, k, False)

        @block.scalar
        def _(act):
            def split(n, k, q, first):
                act.wait_ge(tile_in[k], 16 * q + 16)
                if not first:
                    act.wait_ge(tile_summed, n - 1)
                nc.scalar.activation(high[:, k % 2, :], ring[:, k, :], ACT.Copy).then_inc(high_ready, 1)

            for k in range(RING):
                split(k, k, 0, k < 2)
            with act.Fori(1, SUP * QUADS) as q:
                for k in range(RING):
                    split(q * RING + k, k, q, False)

        @block.vector
        def _(dve):
            def split(n, k, first):
                dve.wait_ge(high_ready, n + 1)
                if not first:
                    dve.wait_ge(tile_summed, n - 1)
                nc.vector.tensor_tensor(low[:, k % 2, :], ring[:, k, :], high[:, k % 2, :].bitcast(F32), ALU.subtract)\
                    .then_inc(low_ready, 1)

            def drain_bank(s, b):
                cols = bass.ds(s * SPAN + b * BANK, BANK)
                if second:
                    nc.vector.scalar_tensor_tensor(out[:, cols], psum[:, b, :], 2.0, xT[:, cols], ALU.mult, ALU.subtract)\
                        .then_inc(bank_free, 1)
                else:
                    nc.vector.tensor_copy(out[:, cols], psum[:, b, :]).then_inc(bank_free, 1)

            def span(s, first):
                for k in range(RING):
                    split(s * (QUADS * RING) + k, k, first and k < 2)
                with dve.Fori(1, QUADS) as q:
                    for k in range(RING):
                        split((s * QUADS + q) * RING + k, k, False)
                dve.wait_ge(tile_summed, s * (QUADS * RING) + QUADS * RING)
                for b in range(BANKS):
                    drain_bank(s, b)

            span(0, True)
            with dve.Fori(1, SUP) as s:
                span(s, False)

        @block.tensor
        def _(pe):
            def tile(s, q, k, start, stop, first):
                n = (s * QUADS + q) * RING + k
                pe.wait_ge(w_ready, n + 1)
                pe.wait_ge(high_ready, n + 1)
                for b in range(BANKS):
                    if start and not first:
                        pe.wait_ge(bank_free, s * BANKS + (b - BANKS + 1))
                    nc.tensor.matmul(psum[:, b, :], w_high[:, k, :], high[:, k % 2, bass.ts(b, BANK)], start=start, stop=False)
                for b in range(BANKS):
                    nc.tensor.matmul(psum[:, b, :], w_low[:, k, :], high[:, k % 2, bass.ts(b, BANK)], start=False, stop=False)
                pe.wait_ge(low_ready, n + 1)
                for b in range(BANKS):
                    last = nc.tensor.matmul(psum[:, b, :], w_high[:, k, :], low[:, k % 2, bass.ts(b, BANK)],
                                            start=False, stop=stop)
                last.then_inc(tile_summed, 1)

            def span(s, first):
                for k in range(RING):
                    tile(s, 0, k, k == 0, False, first)
                with pe.Fori(1, QUADS - 1) as q:
                    for k in range(RING):
                        tile(s, q, k, False, False, False)
                for k in range(RING):
                    tile(s, QUADS - 1, k, False, k == RING - 1, False)

            span(0, True)
            with pe.Fori(1, SUP) as s:
                span(s, False)


def turn(nc, T, mem):
    t1T, nat, ident, psum = mem["t1T"], mem["nat"], mem["ident"], mem["psum"]
    PER = BANK // P
    GROUPS = T // PER
    with (
        nc.semaphore("turned") as turned,
        nc.semaphore("turn_copied") as copied,
        nc.Block() as block,
    ):
        @block.tensor
        def _(pe):
            for g in range(GROUPS):
                if g >= 8:
                    pe.wait_ge(copied, g - 7)
                for k in range(PER):
                    last = nc.tensor.transpose(psum[:, g % 8, bass.ts(k, P)], t1T[:, bass.ts(g * PER + k, P)], ident[:, :])
                last.then_inc(turned, 1)

        @block.vector
        def _(dve):
            for g in range(GROUPS):
                dve.wait_ge(turned, g + 1)
                nc.vector.tensor_copy(nat[:, bass.ts(g, PER), :].rearrange("p a d -> p (a d)"), psum[:, g % 8, :])\
                    .then_inc(copied, 1)


def nodes_stage(nc, T, mem, x1_dram):
    xT, t1T, t2T, nat, psum, ident = (mem[k] for k in ("xT", "t1T", "t2T", "nat", "psum", "ident"))
    w_cheb, w_att, a_r_wide, a_s, b_col = (mem[k] for k in ("w_cheb", "w_att", "a_r_wide", "a_s", "b_col"))
    s_all, half = mem["s_all"], mem["minus_half"]
    PER = BANK // P
    CH = T // PER
    stats, mv, rstd, veps = mem["stats"], mem["mv"], mem["rstd"], mem["veps"]
    COMBO, Y, X1T, HB, RB, HN, SB = 0, 1, 3, 4, 5, 6, 7
    with ExitStack() as ctx:
        def sem(name):
            return ctx.enter_context(nc.semaphore(name))

        def sbuf(name, shape, dtype):
            return ctx.enter_context(nc.sbuf_tensor(name, shape, dtype))

        yT = sbuf("yT", [P, 2, BANK], F32)
        x1T = sbuf("x1T", [P, 2, BANK], F32)
        HT = sbuf("hT", [P, 2, BANK], F32)
        x1 = sbuf("x1", [P, 2, BANK], F32)
        combo_done = sem("combo_done")
        yT_ready = sem("yT_ready")
        y_turned = sem("y_turned")
        n_stats = sem("n_stats")
        n_mv = sem("n_mv")
        n_veps = sem("n_veps")
        n_rstd = sem("n_rstd")
        x1_ready = sem("x1_ready")
        x1_turned = sem("x1_turned")
        x1T_ready = sem("x1T_ready")
        hT_done = sem("hT_done")
        hT_ready = sem("hT_ready")
        proj_done = sem("proj_done")
        r_kept = sem("r_kept")
        h_kept = sem("h_kept")
        stored = [sem(f"x1_stored{k}") for k in range(2)]
        block = ctx.enter_context(nc.Block())
        @block.tensor
        def _(pe):
            def combine(c):
                if c >= 1:
                    pe.wait_ge(yT_ready, c)
                for j, src in enumerate((xT, t1T, t2T)):
                    last = nc.tensor.matmul(psum[:, COMBO, :], w_cheb[:, j, :], src[:, bass.ts(c, BANK)],
                                            start=j == 0, stop=j == 2)
                last.then_inc(combo_done, 1)

            def turn_y(c):
                pe.wait_ge(yT_ready, c + 1)
                if c >= 2:
                    pe.wait_ge(x1_ready, c - 1)
                for k in range(PER):
                    last = nc.tensor.transpose(psum[:, Y + c % 2, bass.ts(k, P)], yT[:, c % 2, bass.ts(k, P)], ident[:, :])
                last.then_inc(y_turned, 1)

            def turn_x1(c):
                pe.wait_ge(x1_ready, c + 1)
                if c >= 1:
                    pe.wait_ge(x1T_ready, c)
                for k in range(PER):
                    last = nc.tensor.transpose(psum[:, X1T, bass.ts(k, P)], x1[:, c % 2, bass.ts(k, P)], ident[:, :])
                last.then_inc(x1_turned, 1)

            def hidden(c):
                pe.wait_ge(x1T_ready, c + 1)
                if c >= 1:
                    pe.wait_ge(hT_ready, c)
                nc.tensor.matmul(psum[:, HB, :], w_att[:, :], x1T[:, c % 2, :], start=True, stop=True).then_inc(hT_done, 1)

            def project(c):
                pe.wait_ge(hT_ready, c + 1)
                if c >= 1:
                    pe.wait_ge(r_kept, c)
                    pe.wait_ge(h_kept, c)
                nc.tensor.matmul(psum[:, RB, :], a_r_wide[:, :], HT[:, c % 2, :], start=True, stop=True)
                for k in range(PER):
                    nc.tensor.transpose(psum[:, HN, bass.ts(k, P)], HT[:, c % 2, bass.ts(k, P)], ident[:, :])
                for k in range(PER):
                    last = nc.tensor.matmul(psum[:, SB, k:k + 1], HT[:, c % 2, bass.ts(k, P)], a_s[:, :], start=True, stop=True)
                last.then_inc(proj_done, 1)

            for i in range(CH + 4):
                for lag, step in ((0, combine), (1, turn_y), (2, turn_x1), (3, hidden), (4, project)):
                    if 0 <= i - lag < CH:
                        step(i - lag)

        @block.vector
        def _(dve):
            def residual(c):
                dve.wait_ge(combo_done, c + 1)
                if c >= 2:
                    dve.wait_ge(y_turned, c - 1)
                nc.vector.tensor_tensor(yT[:, c % 2, :], psum[:, COMBO, :], xT[:, bass.ts(c, BANK)], ALU.add)\
                    .then_inc(yT_ready, 1)

            def norm(c):
                dve.wait_ge(y_turned, c + 1)
                if c >= 1:
                    dve.wait_ge(x1_ready, c)
                y = psum[:, Y + c % 2, :].rearrange("p (a n) -> p a n", a=PER)
                for k in range(PER):
                    nc.vector.bn_stats(stats[:, k, :], y[:, k, :]).then_inc(n_stats, 1)
                dve.wait_ge(n_stats, PER * (c + 1))
                for k in range(PER):
                    nc.vector.bn_aggr(mv[:, k, :], stats[:, k, :]).then_inc(n_mv, 1)
                dve.wait_ge(n_rstd, c + 1)
                if c >= 2:
                    dve.wait_ge(stored[c % 2], 16 * (c // 2))
                    dve.wait_ge(x1_turned, c - 1)
                for k in range(PER):
                    last = nc.vector.tensor_scalar(x1[:, c % 2, bass.ts(k, P)], y[:, k, :], mv[:, k, 0:1], rstd[:, k:k + 1],
                                                   ALU.subtract, ALU.mult)
                last.then_inc(x1_ready, 1)

            def keep(c):
                dve.wait_ge(proj_done, c + 1)
                nc.vector.tensor_copy(nat[:, bass.ts(c, PER), :].rearrange("p a d -> p (a d)"), psum[:, HN, :])
                nc.vector.tensor_scalar(s_all[:, bass.ts(c, PER)], psum[:, SB, 0:PER], -1.0 / MASKED, None, ALU.mult)\
                    .then_inc(h_kept, 1)

            for i in range(CH + 4):
                for lag, step in ((0, residual), (1, norm), (4, keep)):
                    if 0 <= i - lag < CH:
                        step(i - lag)

        @block.gpsimd
        def _(pool):
            for c in range(CH):
                pool.wait_ge(n_mv, PER * (c + 1))
                nc.gpsimd.tensor_scalar(veps[:, 0:PER], mv[:, 0:PER, 1], EPS, None, ALU.add).then_inc(n_veps, 1)
                pool.wait_ge(n_veps, c + 1)
                nc.gpsimd.tensor_tensor(rstd[:, 0:PER], veps[:, 0:PER], half[:, 0:PER], ALU.pow).then_inc(n_rstd, 1)

        @block.scalar
        def _(act):
            def keep_x1T(c):
                act.wait_ge(x1_turned, c + 1)
                if c >= 2:
                    act.wait_ge(hT_done, c - 1)
                nc.scalar.activation(x1T[:, c % 2, :], psum[:, X1T, :], ACT.Copy).then_inc(x1T_ready, 1)

            def keep_hT(c):
                act.wait_ge(hT_done, c + 1)
                if c >= 2:
                    act.wait_ge(proj_done, c - 1)
                nc.scalar.activation(HT[:, c % 2, :], psum[:, HB, :], ACT.Identity, bias=b_col[:, 0:1]).then_inc(hT_ready, 1)

            def keep_r(c):
                act.wait_ge(proj_done, c + 1)
                nc.scalar.activation(xT[:, bass.ts(c, BANK)], psum[:, RB, :], ACT.Copy, scale=-1.0 / MASKED).then_inc(r_kept, 1)

            for i in range(CH + 4):
                for lag, step in ((2, keep_x1T), (3, keep_hT), (4, keep_r)):
                    if 0 <= i - lag < CH:
                        step(i - lag)

        @block.sync
        def _(sp):
            for c in range(CH):
                sp.wait_ge(x1_ready, c + 1)
                sp.dma_start(x1_dram[bass.ts(c, PER), :, :].rearrange("a p d -> p a d"),
                             x1[:, c % 2, :].rearrange("p (a d) -> p a d", a=PER)).then_inc(stored[c % 2], 16)
            for k in range(2):
                sp.wait_ge(stored[k], 16 * ((CH + 1 - k) // 2))


def attend(nc, T, mem, chunks, x1_dram, y_dram):
    R, H, psum, ident, ring = mem["xT"], mem["nat"], mem["psum"], mem["ident"], mem["ring"]
    E = [mem["t1T"], mem["t2T"]]
    s_all, half = mem["s_all"], mem["minus_half"]
    CH = T * P // SPAN
    assert CH <= RING
    GW = 2 * BANK
    GROUPS = T * P // GW
    GPC = SPAN // GW
    PER = GW // P
    mx, neg_max, sums = mem["mx"], mem["neg_max"], mem["sums"]
    total, recip, stats, mv, veps, rstd = (mem[k] for k in ("total", "recip", "stats", "mv", "veps", "rstd"))
    TURN, OUT = 0, 4
    with ExitStack() as ctx:
        def sem(name):
            return ctx.enter_context(nc.semaphore(name))

        def sbuf(name, shape):
            return ctx.enter_context(nc.sbuf_tensor("a_" + name, shape, F32))

        rest = sbuf("rest", [P, 2, SPAN])
        probsT = sbuf("probsT", [P, 2, GW])
        x1, y, normed = sbuf("x1", [P, 2, P]), sbuf("y", [P, 2, P]), sbuf("normed", [P, 2, P])

        products = sem("a_products")
        scored = sem("a_scored")
        slopes = sem("a_slopes")
        rests = sem("a_rests")
        max_ready = sem("a_max_ready")
        probs_ready = sem("a_probs_ready")
        turned = sem("a_turned")
        copied = sem("a_copied")
        group_summed = sem("a_group_summed")
        t_total = sem("a_t_total")
        t_recip = sem("a_t_recip")
        t_y = sem("a_t_y")
        t_stats = sem("a_t_stats")
        t_mv = sem("a_t_mv")
        t_veps = sem("a_t_veps")
        t_rstd = sem("a_t_rstd")
        y_ready = sem("a_y_ready")
        chunk_in = [sem(f"a_chunk_in{c}") for c in range(CH)]
        x1_in = [sem(f"a_x1_in{p}") for p in range(2)]
        y_out = [sem(f"a_y_out{p}") for p in range(2)]
        block = ctx.enter_context(nc.Block())

        def row(t, dram):
            return dram[bass.ds(t, 1), :, :].rearrange("a p d -> (a p) d")

        @block.sync
        def _(sp):
            def load(t, par, first):
                for c in range(CH):
                    if not first or par:
                        sp.wait_ge(rests, (t - 1) * CH + c + 1)
                    sp.dma_start(ring[:, c, :], row(t * CH + c, chunks)).then_inc(chunk_in[c], 16)
                if not first:
                    sp.wait_ge(t_y, t - 1)
                sp.dma_start(x1[:, par, :], row(t, x1_dram)).then_inc(x1_in[par], 16)

            load(0, 0, True)
            load(1, 1, True)
            with sp.Fori(1, T // 2) as h:
                for par in range(2):
                    load(h * 2 + par, par, False)

        @block.scalar
        def _(act):
            def slope(t, c, first):
                act.wait_ge(products, t * CH + c + 1)
                if not first or c >= 2:
                    act.wait_ge(scored, t * CH + c - 1)
                nc.scalar.activation(rest[:, c % 2, :], E[t_par[0]][:, bass.ts(c, SPAN)], ACT.Relu, scale=1.0 - SLOPE)\
                    .then_inc(slopes, 1)

            def exps(t, par, c):
                if c == 0:
                    act.wait_ge(max_ready, t + 1)
                e = E[par][:, bass.ts(c, SPAN)]
                nc.scalar.activation(e, e, ACT.Exp, bias=neg_max[:, par:par + 1],
                                     accum_out=sums[:, par * RING + c:par * RING + c + 1]).then_inc(probs_ready, 1)

            def copy(t, g, first):
                act.wait_ge(turned, t * GROUPS + g + 1)
                if not first or g >= 2:
                    act.wait_ge(group_summed, t * GROUPS + g - 1)
                nc.scalar.activation(probsT[:, g % 2, :],
                                     psum[:, TURN + 2 * (g % 2):TURN + 2 * (g % 2) + 2, :].rearrange("p a n -> p (a n)"),
                                     ACT.Copy).then_inc(copied, 1)

            def tile(t, par, first, ahead):
                t_par[0] = 1 - par
                f = first and par == 0
                for c in range(CH):
                    exps(t, par, c)
                    if ahead:
                        slope(t + 1, c, False)
                    if c:
                        for g in range(GPC * (c - 1), GPC * c):
                            copy(t, g, f)
                for g in range(GPC * (CH - 1), GROUPS):
                    copy(t, g, f)

            t_par = [0]
            for c in range(CH):
                slope(0, c, True)
            tile(0, 0, True, True)
            tile(1, 1, True, True)
            with act.Fori(1, T // 2 - 1) as h:
                for par in range(2):
                    tile(h * 2 + par, par, False, True)
            tile(T - 2, 0, False, True)
            tile(T - 1, 1, False, False)

        @block.vector
        def _(dve):
            def scores(t, par, first):
                def product(c):
                    dve.wait_ge(chunk_in[c], 16 * t + 16)
                    if not first:
                        dve.wait_ge(turned, (t - 2) * GROUPS + GPC * (c + 1))
                    nc.vector.scalar_tensor_tensor(E[par][:, bass.ts(c, SPAN)], R[:, bass.ts(c, SPAN)], s_all[:, bass.ds(t, 1)],
                                                   ring[:, c, :], ALU.add, ALU.mult).then_inc(products, 1)

                def mask(c):
                    dve.wait_ge(slopes, t * CH + c + 1)
                    nc.vector.scalar_tensor_tensor(rest[:, c % 2, :], ring[:, c, :], 0.0, rest[:, c % 2, :],
                                                   ALU.is_le, ALU.subtract).then_inc(rests, 1)

                def score(c):
                    e = E[par][:, bass.ts(c, SPAN)]
                    wait_alone(dve, rests, t * CH + c + 1)
                    nc.vector.tensor_tensor_reduce(e, e, rest[:, c % 2, :], -MASKED, LOWEST, ALU.add, ALU.max,
                                                   accum_out=mx[:, par * RING + c:par * RING + c + 1]).then_inc(scored, 1)

                for c in range(CH):
                    product(c)
                    if c:
                        mask(c - 1)
                        score(c - 1)
                mask(CH - 1)
                score(CH - 1)
                dve.wait_ge(scored, t * CH + CH)
                if not first:
                    dve.wait_ge(probs_ready, (t - 1) * CH)
                nc.vector.tensor_reduce(neg_max[:, par:par + 1], mx[:, par * RING:par * RING + CH], AX.X, ALU.max,
                                        negate=True).then_inc(max_ready, 1)

            def finish(t, par, free):
                dve.wait_ge(probs_ready, (t + 1) * CH)
                nc.vector.reduce_sum(total[:, par:par + 1], sums[:, par * RING:par * RING + CH], AX.X).then_inc(t_total, 1)
                dve.wait_ge(t_total, t + 1)
                nc.vector.reciprocal(recip[:, par:par + 1], total[:, par:par + 1]).then_inc(t_recip, 1)
                dve.wait_ge(group_summed, (t + 1) * GROUPS)
                dve.wait_ge(x1_in[par], 16 * half_of(t, par) + 16)
                dve.wait_ge(t_recip, t + 1)
                nc.vector.scalar_tensor_tensor(y[:, par, :], psum[:, OUT + par, 0:P], recip[:, par:par + 1], x1[:, par, :],
                                               ALU.mult, ALU.add).then_inc(t_y, 1)
                dve.wait_ge(t_y, t + 1)
                nc.vector.bn_stats(stats[:, par, :], y[:, par, :]).then_inc(t_stats, 1)
                wait_alone(dve, t_stats, t + 1)
                nc.vector.bn_aggr(mv[:, par, :], stats[:, par, :]).then_inc(t_mv, 1)
                dve.wait_ge(t_mv, t + 1)
                nc.vector.tensor_scalar(veps[:, par:par + 1], mv[:, par, 1:2], EPS, None, ALU.add).then_inc(t_veps, 1)
                dve.wait_ge(t_rstd, t + 1)
                if free:
                    dve.wait_ge(y_out[par], 16 * half_of(t, par))
                nc.vector.tensor_scalar(normed[:, par, :], y[:, par, :], mv[:, par, 0:1], rstd[:, par:par + 1],
                                        ALU.subtract, ALU.mult).then_inc(y_ready, 1)

            def half_of(t, par):
                return (t - par) // 2 if isinstance(t, int) else pair[0] - 1

            pair = [None]
            scores(0, 0, True)
            scores(1, 1, True)
            finish(0, 0, False)
            scores(2, 0, False)
            finish(1, 1, False)
            scores(3, 1, False)
            with dve.Fori(2, T // 2) as h:
                pair[0] = h
                for par in range(2):
                    finish(h * 2 + (par - 2), par, True)
                    scores(h * 2 + par, par, False)
            for t in (T - 2, T - 1):
                finish(t, t % 2, True)

        @block.gpsimd
        def _(pool):
            def rstd_of(t, par):
                pool.wait_ge(t_veps, t + 1)
                nc.gpsimd.tensor_tensor(rstd[:, par:par + 1], veps[:, par:par + 1], half[:, 0:1], ALU.pow).then_inc(t_rstd, 1)
                pool.wait_ge(y_ready, t + 1)
                pool.dma_start(row(t, y_dram), normed[:, par, :]).then_inc(y_out[par], 16)

            with pool.Fori(0, T // 2) as h:
                for par in range(2):
                    rstd_of(h * 2 + par, par)
            for par in range(2):
                pool.wait_ge(y_out[par], 16 * (T // 2))

        @block.tensor
        def _(pe):
            def turn_group(t, par, g, first):
                pe.wait_ge(probs_ready, t * CH + g // GPC + 1)
                if not first or g >= 2:
                    pe.wait_ge(copied, t * GROUPS + g - 1)
                for k in range(PER):
                    last = nc.tensor.transpose(
                        psum[:, TURN + 2 * (g % 2) + k // (PER // 2), bass.ts(k % (PER // 2), P)],
                        E[par][:, bass.ts(g * PER + k, P)], ident[:, :])
                last.then_inc(turned, 1)

            def sum_group(t, par, g, free):
                pe.wait_ge(copied, t * GROUPS + g + 1)
                if g == 0 and free:
                    pe.wait_ge(t_y, t - 1)
                for k in range(PER):
                    last = nc.tensor.matmul(psum[:, OUT + par, 0:P], probsT[:, g % 2, bass.ts(k, P)], H[:, g * PER + k, :],
                                            start=(g == 0 and k == 0), stop=(g == GROUPS - 1 and k == PER - 1))
                last.then_inc(group_summed, 1)

            def tile(t, par, first):
                f = first and par == 0
                turn_group(t, par, 0, f)
                for g in range(GROUPS):
                    if g + 1 < GROUPS:
                        turn_group(t, par, g + 1, f)
                    sum_group(t, par, g, not first)

            tile(0, 0, True)
            tile(1, 1, True)
            with pe.Fori(1, T // 2) as h:
                for par in range(2):
                    tile(h * 2 + par, par, False)


def load_and_prepare(nc, T, mem, xn, xT, w_cheb, w_att, b, a_s, a_r, ident):
    with (
        nc.semaphore("loaded") as loaded, nc.semaphore("ones_set") as ones_set,
        nc.semaphore("prepared") as prepared,
        nc.Block() as block,
    ):
        @block.sync
        def _(sp):
            for dst, src in ((mem["nat"][:, :, :], xn), (mem["xT"][:, :], xT), (mem["w_cheb"][:, :, :], w_cheb),
                             (mem["w_att"][:, :], w_att), (mem["b_col"][:, :], b), (mem["a_s"][:, :], a_s),
                             (mem["a_r"][:, :], a_r), (mem["ident"][:, :], ident)):
                sp.dma_start(dst, src).then_inc(loaded, 16)
            sp.wait_ge(loaded, 16 * 8)

        @block.vector
        def _(dve):
            nc.vector.memset(mem["a_r_wide"][:, :], 1.0).then_inc(ones_set, 1)
            nc.vector.memset(mem["minus_half"][:, :], -0.5)
            dve.wait_ge(ones_set, 1)
            dve.wait_ge(loaded, 16 * 8)
            nc.vector.tensor_scalar(mem["a_r_wide"][:, :], mem["a_r_wide"][:, :], mem["a_r"][:, 0:1], None, ALU.mult)\
                .then_inc(prepared, 1)


def build(nc, tilesT, tiles, xn, xT, w_cheb, w_att, b, a_s, a_r, ident, y):
    T = xn.shape[1]
    x1_dram = nc.dram_tensor("x1_rows", (T, P, P), F32, kind="Internal").ap()
    shapes = {
        "nat": ([P, T, P], F32), "xT": ([P, T * P], F32), "t1T": ([P, T * P], F32), "t2T": ([P, T * P], F32),
        "ring": ([P, RING, SPAN], F32),
        "w_cheb": ([P, 3, P], F32), "w_att": ([P, P], F32), "ident": ([P, P], F32), "a_r_wide": ([P, P], F32),
        "b_col": ([P, 1], F32), "a_s": ([P, 1], F32), "a_r": ([P, 1], F32), "minus_half": ([P, 4], F32),
        "s_all": ([P, T], F32), "stats": ([P, 4, 6], F32), "mv": ([P, 4, 2], F32), "veps": ([P, 4], F32),
        "rstd": ([P, 4], F32), "mx": ([P, 2 * RING], F32), "sums": ([P, 2 * RING], F32),
        "neg_max": ([P, 2], F32), "total": ([P, 2], F32), "recip": ([P, 2], F32),
    }
    with ExitStack() as ctx:
        mem = {k: ctx.enter_context(nc.sbuf_tensor("sb_" + k, s, d)) for k, (s, d) in shapes.items()}
        mem["psum"] = ctx.enter_context(nc.psum_tensor("psum", [P, 8, BANK], F32))
        load_and_prepare(nc, T, mem, xn, xT, w_cheb, w_att, b, a_s, a_r, ident)
        diffuse(nc, "d1", tilesT, T, mem["nat"], mem, False)
        turn(nc, T, mem)
        diffuse(nc, "d2", tilesT, T, mem["nat"], mem, True)
        nodes_stage(nc, T, mem, x1_dram)
        attend(nc, T, mem, tiles, x1_dram, y)


def layouts(x, adj, L0_gnn_W, L1_gnn_W, L1_gnn_b, L1_gnn_a_s, L1_gnn_a_r):
    N = x.shape[0]
    T, S = N // P, N // SPAN
    c = np.ascontiguousarray
    return {
        "tilesT": c(adj.reshape(S, SPAN, T, P).transpose(0, 2, 3, 1)).reshape(S * T, P, SPAN),
        "tiles": c(adj.reshape(T, P, S, SPAN).transpose(0, 2, 1, 3)).reshape(T * S, P, SPAN),
        "xn": c(x.reshape(T, P, P).transpose(1, 0, 2)),
        "xT": c(x.T),
        "w_cheb": c(L0_gnn_W.transpose(2, 0, 1)),
        "w_att": c(L1_gnn_W.T),
        "b": c(L1_gnn_b.reshape(P, 1)),
        "a_s": c(L1_gnn_a_s), "a_r": c(L1_gnn_a_r),
        "ident": np.eye(P, dtype=np.float32),
    }


def kernel(x, adj, L0_gnn_W, L1_gnn_W, L1_gnn_b, L1_gnn_a_s, L1_gnn_a_r):
    import concourse.bacc as bacc
    from concourse.bass_utils import run_bass_kernel_spmd

    args = [np.asarray(a) for a in (x, adj, L0_gnn_W, L1_gnn_W, L1_gnn_b, L1_gnn_a_s, L1_gnn_a_r)]
    arrays = layouts(*args)
    N = args[0].shape[0]
    nc = bacc.Bacc("TRN2", target_bir_lowering=False, num_devices=1)
    aps = [nc.dram_tensor(k, a.shape, mybir.dt.from_np(a.dtype), kind="ExternalInput").ap() for k, a in arrays.items()]
    y = nc.dram_tensor("y", (N // P, P, P), F32, kind="ExternalOutput").ap()
    build(nc, *aps, y)
    r = run_bass_kernel_spmd(nc, [arrays], core_ids=[0])
    return r.results[0]["y"].reshape(N, P)
```

```python
from contextlib import ExitStack

import numpy as np
import concourse.bass as bass
from concourse import mybir

P = 128
BANK = 512
SPAN = 2048
RING = 4
MASKED = 2.0 ** 53
LOWEST = -3.0e38
SLOPE = 0.2
EPS = 1e-5

F32 = mybir.dt.float32
F32R = mybir.dt.float32r
ALU = mybir.AluOpType
ACT = mybir.ActivationFunctionType
AX = mybir.AxisListType


def wait_alone(engine, semaphore, value):
    engine.wait_ge(semaphore, 1)
    engine.wait_ge(semaphore, value)


def diffuse(nc, name, tiles, T, nodes, mem, second):
    SUP = T * P // SPAN
    QUADS = T // RING
    BANKS = SPAN // BANK
    ring, psum = mem["ring"], mem["psum"]
    out, xT = mem["t2T" if second else "t1T"], mem["xT"]
    with ExitStack() as ctx:
        def sem(name):
            return ctx.enter_context(nc.semaphore(name))

        def sbuf(name, shape, dtype):
            return ctx.enter_context(nc.sbuf_tensor(name, shape, dtype))

        high = sbuf(name + "_high", [P, 2, SPAN], F32R)
        low = sbuf(name + "_low", [P, 2, SPAN], F32R)
        w_high = sbuf(name + "_w_high", [P, RING, P], F32R)
        w_low = sbuf(name + "_w_low", [P, RING, P], F32R)
        tile_in = [sem(f"{name}_tile_in{k}") for k in range(RING)]
        high_ready = sem(name + "_high_ready")
        low_ready = sem(name + "_low_ready")
        w_full = sbuf(name + "_w_full", [P, RING, P], F32)
        w_copied = sem(name + "_w_copied")
        w_ready = sem(name + "_w_ready")
        tile_summed = sem(name + "_tile_summed")
        bank_free = sem(name + "_bank_free")
        block = ctx.enter_context(nc.Block())
        @block.sync
        def _(sp):
            for k in range(RING):
                sp.dma_start(ring[:, k, :], tiles[k, :, :]).then_inc(tile_in[k], 16)
            with sp.Fori(1, SUP * QUADS) as q:
                for k in range(RING):
                    sp.wait_ge(low_ready, q * RING + (k - RING + 1))
                    sp.dma_start(ring[:, k, :], tiles[bass.ds(q * RING + k, 1), :, :].rearrange("a p n -> (a p) n"))\
                        .then_inc(tile_in[k], 16)

        @block.gpsimd
        def _(pool):
            def split(s, q, k, first):
                n = (s * QUADS + q) * RING + k
                if not first:
                    pool.wait_ge(tile_summed, n - (RING - 1))
                src = nodes[:, bass.ds(q * RING + k, 1), :].rearrange("p a d -> p (a d)")
                nc.gpsimd.tensor_copy(w_full[:, k, :], src).then_inc(w_copied, 1)
                nc.gpsimd.tensor_copy(w_high[:, k, :], src).then_inc(w_copied, 1)
                pool.wait_ge(w_copied, 2 * n + 2)
                nc.gpsimd.tensor_tensor(w_low[:, k, :], w_full[:, k, :], w_high[:, k, :].bitcast(F32), ALU.subtract)\
                    .then_inc(w_ready, 1)

            for k in range(RING):
                split(0, 0, k, True)
            with pool.Fori(1, QUADS) as q:
                for k in range(RING):
                    split(0, q, k, False)
            with pool.Fori(1, SUP) as s:
                with pool.Fori(0, QUADS) as q:
                    for k in range(RING):
                        split(s, q, k, False)

        @block.scalar
        def _(act):
            def split(n, k, q, first):
                act.wait_ge(tile_in[k], 16 * q + 16)
                if not first:
                    act.wait_ge(tile_summed, n - 1)
                nc.scalar.activation(high[:, k % 2, :], ring[:, k, :], ACT.Copy).then_inc(high_ready, 1)

            for k in range(RING):
                split(k, k, 0, k < 2)
            with act.Fori(1, SUP * QUADS) as q:
                for k in range(RING):
                    split(q * RING + k, k, q, False)

        @block.vector
        def _(dve):
            def split(n, k, first):
                dve.wait_ge(high_ready, n + 1)
                if not first:
                    dve.wait_ge(tile_summed, n - 1)
                nc.vector.tensor_tensor(low[:, k % 2, :], ring[:, k, :], high[:, k % 2, :].bitcast(F32), ALU.subtract)\
                    .then_inc(low_ready, 1)

            def drain_bank(s, b):
                cols = bass.ds(s * SPAN + b * BANK, BANK)
                if second:
                    nc.vector.scalar_tensor_tensor(out[:, cols], psum[:, b, :], 2.0, xT[:, cols], ALU.mult, ALU.subtract)\
                        .then_inc(bank_free, 1)
                else:
                    nc.vector.tensor_copy(out[:, cols], psum[:, b, :]).then_inc(bank_free, 1)

            def span(s, first):
                for k in range(RING):
                    split(s * (QUADS * RING) + k, k, first and k < 2)
                with dve.Fori(1, QUADS) as q:
                    for k in range(RING):
                        split((s * QUADS + q) * RING + k, k, False)
                dve.wait_ge(tile_summed, s * (QUADS * RING) + QUADS * RING)
                for b in range(BANKS):
                    drain_bank(s, b)

            span(0, True)
            with dve.Fori(1, SUP) as s:
                span(s, False)

        @block.tensor
        def _(pe):
            def tile(s, q, k, start, stop, first):
                n = (s * QUADS + q) * RING + k
                pe.wait_ge(w_ready, n + 1)
                pe.wait_ge(high_ready, n + 1)
                for b in range(BANKS):
                    if start and not first:
                        pe.wait_ge(bank_free, s * BANKS + (b - BANKS + 1))
                    nc.tensor.matmul(psum[:, b, :], w_high[:, k, :], high[:, k % 2, bass.ts(b, BANK)], start=start, stop=False)
                for b in range(BANKS):
                    nc.tensor.matmul(psum[:, b, :], w_low[:, k, :], high[:, k % 2, bass.ts(b, BANK)], start=False, stop=False)
                pe.wait_ge(low_ready, n + 1)
                for b in range(BANKS):
                    last = nc.tensor.matmul(psum[:, b, :], w_high[:, k, :], low[:, k % 2, bass.ts(b, BANK)],
                                            start=False, stop=stop)
                last.then_inc(tile_summed, 1)

            def span(s, first):
                for k in range(RING):
                    tile(s, 0, k, k == 0, False, first)
                with pe.Fori(1, QUADS - 1) as q:
                    for k in range(RING):
                        tile(s, q, k, False, False, False)
                for k in range(RING):
                    tile(s, QUADS - 1, k, False, k == RING - 1, False)

            span(0, True)
            with pe.Fori(1, SUP) as s:
                span(s, False)


def turn(nc, T, mem):
    t1T, nat, ident, psum = mem["t1T"], mem["nat"], mem["ident"], mem["psum"]
    PER = BANK // P
    GROUPS = T // PER
    with (
        nc.semaphore("turned") as turned,
        nc.semaphore("turn_copied") as copied,
        nc.Block() as block,
    ):
        @block.tensor
        def _(pe):
            for g in range(GROUPS):
                if g >= 8:
                    pe.wait_ge(copied, g - 7)
                for k in range(PER):
                    last = nc.tensor.transpose(psum[:, g % 8, bass.ts(k, P)], t1T[:, bass.ts(g * PER + k, P)], ident[:, :])
                last.then_inc(turned, 1)

        @block.vector
        def _(dve):
            for g in range(GROUPS):
                dve.wait_ge(turned, g + 1)
                nc.vector.tensor_copy(nat[:, bass.ts(g, PER), :].rearrange("p a d -> p (a d)"), psum[:, g % 8, :])\
                    .then_inc(copied, 1)


def nodes_stage(nc, T, mem, x1_dram):
    xT, t1T, t2T, nat, psum, ident = (mem[k] for k in ("xT", "t1T", "t2T", "nat", "psum", "ident"))
    w_cheb, w_att, a_r_wide, a_s, b_col = (mem[k] for k in ("w_cheb", "w_att", "a_r_wide", "a_s", "b_col"))
    s_all, half = mem["s_all"], mem["minus_half"]
    PER = BANK // P
    CH = T // PER
    stats, mv, rstd, veps = mem["stats"], mem["mv"], mem["rstd"], mem["veps"]
    COMBO, Y, X1T, HB, RB, HN, SB = 0, 1, 3, 4, 5, 6, 7
    with ExitStack() as ctx:
        def sem(name):
            return ctx.enter_context(nc.semaphore(name))

        def sbuf(name, shape, dtype):
            return ctx.enter_context(nc.sbuf_tensor(name, shape, dtype))

        yT = sbuf("yT", [P, 2, BANK], F32)
        x1T = sbuf("x1T", [P, 2, BANK], F32)
        HT = sbuf("hT", [P, 2, BANK], F32)
        x1 = sbuf("x1", [P, 2, BANK], F32)
        combo_done = sem("combo_done")
        yT_ready = sem("yT_ready")
        y_turned = sem("y_turned")
        n_stats = sem("n_stats")
        n_mv = sem("n_mv")
        n_veps = sem("n_veps")
        n_rstd = sem("n_rstd")
        x1_ready = sem("x1_ready")
        x1_turned = sem("x1_turned")
        x1T_ready = sem("x1T_ready")
        hT_done = sem("hT_done")
        hT_ready = sem("hT_ready")
        proj_done = sem("proj_done")
        r_kept = sem("r_kept")
        h_kept = sem("h_kept")
        stored = [sem(f"x1_stored{k}") for k in range(2)]
        block = ctx.enter_context(nc.Block())
        @block.tensor
        def _(pe):
            def combine(c):
                if c >= 1:
                    pe.wait_ge(yT_ready, c)
                for j, src in enumerate((xT, t1T, t2T)):
                    last = nc.tensor.matmul(psum[:, COMBO, :], w_cheb[:, j, :], src[:, bass.ts(c, BANK)],
                                            start=j == 0, stop=j == 2)
                last.then_inc(combo_done, 1)

            def turn_y(c):
                pe.wait_ge(yT_ready, c + 1)
                if c >= 2:
                    pe.wait_ge(x1_ready, c - 1)
                for k in range(PER):
                    last = nc.tensor.transpose(psum[:, Y + c % 2, bass.ts(k, P)], yT[:, c % 2, bass.ts(k, P)], ident[:, :])
                last.then_inc(y_turned, 1)

            def turn_x1(c):
                pe.wait_ge(x1_ready, c + 1)
                if c >= 1:
                    pe.wait_ge(x1T_ready, c)
                for k in range(PER):
                    last = nc.tensor.transpose(psum[:, X1T, bass.ts(k, P)], x1[:, c % 2, bass.ts(k, P)], ident[:, :])
                last.then_inc(x1_turned, 1)

            def hidden(c):
                pe.wait_ge(x1T_ready, c + 1)
                if c >= 1:
                    pe.wait_ge(hT_ready, c)
                nc.tensor.matmul(psum[:, HB, :], w_att[:, :], x1T[:, c % 2, :], start=True, stop=True).then_inc(hT_done, 1)

            def project(c):
                pe.wait_ge(hT_ready, c + 1)
                if c >= 1:
                    pe.wait_ge(r_kept, c)
                    pe.wait_ge(h_kept, c)
                nc.tensor.matmul(psum[:, RB, :], a_r_wide[:, :], HT[:, c % 2, :], start=True, stop=True)
                for k in range(PER):
                    nc.tensor.transpose(psum[:, HN, bass.ts(k, P)], HT[:, c % 2, bass.ts(k, P)], ident[:, :])
                for k in range(PER):
                    last = nc.tensor.matmul(psum[:, SB, k:k + 1], HT[:, c % 2, bass.ts(k, P)], a_s[:, :], start=True, stop=True)
                last.then_inc(proj_done, 1)

            for i in range(CH + 4):
                for lag, step in ((0, combine), (1, turn_y), (2, turn_x1), (3, hidden), (4, project)):
                    if 0 <= i - lag < CH:
                        step(i - lag)

        @block.vector
        def _(dve):
            def residual(c):
                dve.wait_ge(combo_done, c + 1)
                if c >= 2:
                    dve.wait_ge(y_turned, c - 1)
                nc.vector.tensor_tensor(yT[:, c % 2, :], psum[:, COMBO, :], xT[:, bass.ts(c, BANK)], ALU.add)\
                    .then_inc(yT_ready, 1)

            def norm(c):
                dve.wait_ge(y_turned, c + 1)
                if c >= 1:
                    dve.wait_ge(x1_ready, c)
                y = psum[:, Y + c % 2, :].rearrange("p (a n) -> p a n", a=PER)
                for k in range(PER):
                    nc.vector.bn_stats(stats[:, k, :], y[:, k, :]).then_inc(n_stats, 1)
                dve.wait_ge(n_stats, PER * (c + 1))
                for k in range(PER):
                    nc.vector.bn_aggr(mv[:, k, :], stats[:, k, :]).then_inc(n_mv, 1)
                dve.wait_ge(n_rstd, c + 1)
                if c >= 2:
                    dve.wait_ge(stored[c % 2], 16 * (c // 2))
                    dve.wait_ge(x1_turned, c - 1)
                for k in range(PER):
                    last = nc.vector.tensor_scalar(x1[:, c % 2, bass.ts(k, P)], y[:, k, :], mv[:, k, 0:1], rstd[:, k:k + 1],
                                                   ALU.subtract, ALU.mult)
                last.then_inc(x1_ready, 1)

            def keep(c):
                dve.wait_ge(proj_done, c + 1)
                nc.vector.tensor_copy(nat[:, bass.ts(c, PER), :].rearrange("p a d -> p (a d)"), psum[:, HN, :])
                nc.vector.tensor_scalar(s_all[:, bass.ts(c, PER)], psum[:, SB, 0:PER], -1.0 / MASKED, None, ALU.mult)\
                    .then_inc(h_kept, 1)

            for i in range(CH + 4):
                for lag, step in ((0, residual), (1, norm), (4, keep)):
                    if 0 <= i - lag < CH:
                        step(i - lag)

        @block.gpsimd
        def _(pool):
            for c in range(CH):
                pool.wait_ge(n_mv, PER * (c + 1))
                nc.gpsimd.tensor_scalar(veps[:, 0:PER], mv[:, 0:PER, 1], EPS, None, ALU.add).then_inc(n_veps, 1)
                pool.wait_ge(n_veps, c + 1)
                nc.gpsimd.tensor_tensor(rstd[:, 0:PER], veps[:, 0:PER], half[:, 0:PER], ALU.pow).then_inc(n_rstd, 1)

        @block.scalar
        def _(act):
            def keep_x1T(c):
                act.wait_ge(x1_turned, c + 1)
                if c >= 2:
                    act.wait_ge(hT_done, c - 1)
                nc.scalar.activation(x1T[:, c % 2, :], psum[:, X1T, :], ACT.Copy).then_inc(x1T_ready, 1)

            def keep_hT(c):
                act.wait_ge(hT_done, c + 1)
                if c >= 2:
                    act.wait_ge(proj_done, c - 1)
                nc.scalar.activation(HT[:, c % 2, :], psum[:, HB, :], ACT.Identity, bias=b_col[:, 0:1]).then_inc(hT_ready, 1)

            def keep_r(c):
                act.wait_ge(proj_done, c + 1)
                nc.scalar.activation(xT[:, bass.ts(c, BANK)], psum[:, RB, :], ACT.Copy, scale=-1.0 / MASKED).then_inc(r_kept, 1)

            for i in range(CH + 4):
                for lag, step in ((2, keep_x1T), (3, keep_hT), (4, keep_r)):
                    if 0 <= i - lag < CH:
                        step(i - lag)

        @block.sync
        def _(sp):
            for c in range(CH):
                sp.wait_ge(x1_ready, c + 1)
                sp.dma_start(x1_dram[bass.ts(c, PER), :, :].rearrange("a p d -> p a d"),
                             x1[:, c % 2, :].rearrange("p (a d) -> p a d", a=PER)).then_inc(stored[c % 2], 16)
            for k in range(2):
                sp.wait_ge(stored[k], 16 * ((CH + 1 - k) // 2))


def attend(nc, T, mem, chunks, x1_dram, y_dram):
    R, H, psum, ident, ring = mem["xT"], mem["nat"], mem["psum"], mem["ident"], mem["ring"]
    E = [mem["t1T"], mem["t2T"]]
    s_all, half = mem["s_all"], mem["minus_half"]
    CH = T * P // SPAN
    assert CH <= RING
    GW = 2 * BANK
    GROUPS = T * P // GW
    GPC = SPAN // GW
    PER = GW // P
    mx, neg_max, sums = mem["mx"], mem["neg_max"], mem["sums"]
    total, recip, stats, mv, veps, rstd = (mem[k] for k in ("total", "recip", "stats", "mv", "veps", "rstd"))
    TURN, OUT = 0, 4
    with ExitStack() as ctx:
        def sem(name):
            return ctx.enter_context(nc.semaphore(name))

        def sbuf(name, shape):
            return ctx.enter_context(nc.sbuf_tensor("a_" + name, shape, F32))

        rest = sbuf("rest", [P, 2, SPAN])
        probsT = sbuf("probsT", [P, 2, GW])
        x1, y, normed = sbuf("x1", [P, 2, P]), sbuf("y", [P, 2, P]), sbuf("normed", [P, 2, P])

        products = sem("a_products")
        scored = sem("a_scored")
        slopes = sem("a_slopes")
        rests = sem("a_rests")
        max_ready = sem("a_max_ready")
        probs_ready = sem("a_probs_ready")
        turned = sem("a_turned")
        copied = sem("a_copied")
        group_summed = sem("a_group_summed")
        t_total = sem("a_t_total")
        t_recip = sem("a_t_recip")
        t_y = sem("a_t_y")
        t_stats = sem("a_t_stats")
        t_mv = sem("a_t_mv")
        t_veps = sem("a_t_veps")
        t_rstd = sem("a_t_rstd")
        y_ready = sem("a_y_ready")
        chunk_in = [sem(f"a_chunk_in{c}") for c in range(CH)]
        x1_in = [sem(f"a_x1_in{p}") for p in range(2)]
        y_out = [sem(f"a_y_out{p}") for p in range(2)]
        block = ctx.enter_context(nc.Block())

        def row(t, dram):
            return dram[bass.ds(t, 1), :, :].rearrange("a p d -> (a p) d")

        @block.sync
        def _(sp):
            def load(t, par, first):
                for c in range(CH):
                    if not first or par:
                        sp.wait_ge(rests, (t - 1) * CH + c + 1)
                    sp.dma_start(ring[:, c, :], row(t * CH + c, chunks)).then_inc(chunk_in[c], 16)

            load(0, 0, True)
            load(1, 1, True)
            with sp.Fori(1, T // 2) as h:
                for par in range(2):
                    load(h * 2 + par, par, False)

        @block.scalar
        def _(act):
            def slope(t, par, c, first):
                act.wait_ge(products, t * CH + c + 1)
                if not first or c >= 2:
                    act.wait_ge(scored, t * CH + c - 1)
                nc.scalar.activation(rest[:, c % 2, :], E[par][:, bass.ts(c, SPAN)], ACT.Relu, scale=1.0 - SLOPE)\
                    .then_inc(slopes, 1)

            def exps(t, par, c):
                if c == 0:
                    act.wait_ge(max_ready, t + 1)
                e = E[par][:, bass.ts(c, SPAN)]
                nc.scalar.activation(e, e, ACT.Exp, bias=neg_max[:, par:par + 1],
                                     accum_out=sums[:, par * RING + c:par * RING + c + 1]).then_inc(probs_ready, 1)

            def copy(t, g, first):
                act.wait_ge(turned, t * GROUPS + g + 1)
                if not first or g >= 2:
                    act.wait_ge(group_summed, t * GROUPS + g - 1)
                nc.scalar.activation(probsT[:, g % 2, :],
                                     psum[:, TURN + 2 * (g % 2):TURN + 2 * (g % 2) + 2, :].rearrange("p a n -> p (a n)"),
                                     ACT.Copy).then_inc(copied, 1)

            def tile(t, par, first, ahead):
                for c in range(CH):
                    if ahead:
                        slope(t + 1, 1 - par, c, False)
                    exps(t, par, c)
                    if c:
                        for g in range(GPC * (c - 1), GPC * c):
                            copy(t, g, first and par == 0)
                    elif not first or par:
                        for g in range(GPC * (CH - 1), GROUPS):
                            copy(t - 1, g, False)

            for c in range(CH):
                slope(0, 0, c, True)
            tile(0, 0, True, True)
            tile(1, 1, True, True)
            with act.Fori(1, T // 2 - 1) as h:
                for par in range(2):
                    tile(h * 2 + par, par, False, True)
            tile(T - 2, 0, False, True)
            tile(T - 1, 1, False, False)
            for g in range(GPC * (CH - 1), GROUPS):
                copy(T - 1, g, False)

        @block.vector
        def _(dve):
            def product(t, par, c, first):
                n = t * CH + c
                dve.wait_ge(chunk_in[c], 16 * t + 16)
                if not first:
                    dve.wait_ge(turned, (t - 2) * GROUPS + GPC * (c + 1))
                nc.vector.scalar_tensor_tensor(E[par][:, bass.ts(c, SPAN)], R[:, bass.ts(c, SPAN)], s_all[:, bass.ds(t, 1)],
                                               ring[:, c, :], ALU.add, ALU.mult).then_inc(products, 1)

            def mask(t, c):
                dve.wait_ge(slopes, t * CH + c + 1)
                nc.vector.scalar_tensor_tensor(rest[:, c % 2, :], ring[:, c, :], 0.0, rest[:, c % 2, :],
                                               ALU.is_le, ALU.subtract).then_inc(rests, 1)

            def score(t, par, c):
                e = E[par][:, bass.ts(c, SPAN)]
                wait_alone(dve, rests, t * CH + c + 1)
                nc.vector.tensor_tensor_reduce(e, e, rest[:, c % 2, :], -MASKED, LOWEST, ALU.add, ALU.max,
                                               accum_out=mx[:, par * RING + c:par * RING + c + 1]).then_inc(scored, 1)

            def maximum(t, par, first):
                dve.wait_ge(scored, t * CH + CH)
                if not first:
                    dve.wait_ge(probs_ready, (t - 1) * CH)
                nc.vector.tensor_reduce(neg_max[:, par:par + 1], mx[:, par * RING:par * RING + CH], AX.X, ALU.max,
                                        negate=True).then_inc(max_ready, 1)

            def finish(t, u, par, free):
                one = slice(par, par + 1)

                def add_totals():
                    dve.wait_ge(probs_ready, (t + 1) * CH)
                    nc.vector.reduce_sum(total[:, one], sums[:, par * RING:par * RING + CH], AX.X).then_inc(t_total, 1)

                def invert():
                    dve.wait_ge(t_total, t + 1)
                    nc.vector.reciprocal(recip[:, one], total[:, one]).then_inc(t_recip, 1)

                def residual():
                    dve.wait_ge(group_summed, (t + 1) * GROUPS)
                    dve.wait_ge(x1_in[par], 16 * u + 16)
                    dve.wait_ge(t_recip, t + 1)
                    nc.vector.scalar_tensor_tensor(y[:, par, :], psum[:, OUT + par, 0:P], recip[:, one], x1[:, par, :],
                                                   ALU.mult, ALU.add).then_inc(t_y, 1)

                def moments():
                    dve.wait_ge(t_y, t + 1)
                    nc.vector.bn_stats(stats[:, par, :], y[:, par, :]).then_inc(t_stats, 1)

                def mean_and_variance():
                    wait_alone(dve, t_stats, t + 1)
                    nc.vector.bn_aggr(mv[:, par, :], stats[:, par, :]).then_inc(t_mv, 1)

                def add_eps():
                    dve.wait_ge(t_mv, t + 1)
                    nc.vector.tensor_scalar(veps[:, one], mv[:, par, 1:2], EPS, None, ALU.add).then_inc(t_veps, 1)

                def norm():
                    dve.wait_ge(t_rstd, t + 1)
                    if free:
                        dve.wait_ge(y_out[par], 16 * u)
                    nc.vector.tensor_scalar(normed[:, par, :], y[:, par, :], mv[:, par, 0:1], rstd[:, one],
                                            ALU.subtract, ALU.mult).then_inc(y_ready, 1)

                return [add_totals, invert, residual, moments, mean_and_variance, add_eps, norm]

            def tile(t, par, u, first, last, finishing, free):
                steps = finish(t - 2, u - 1, par, free) if finishing else []
                slot = 0
                for c in range(CH):
                    for work in (mask, product, score):
                        if work is mask:
                            mask(t, c)
                        elif work is score:
                            score(t, par, c)
                        elif c + 2 < CH:
                            product(t, par, c + 2, first)
                        elif not last:
                            product(t + 1, 1 - par, c + 2 - CH, first and par == 0)
                        slot += 1
                        if steps and slot > 3 * (CH // 2 - 1) and (len(steps) > 1 or slot == 3 * CH):
                            steps.pop(0)()
                for step in steps:
                    step()
                maximum(t, par, first)

            for c in range(2):
                product(0, 0, c, True)
            tile(0, 0, 0, True, False, False, False)
            tile(1, 1, 0, True, False, False, False)
            tile(2, 0, 1, False, False, True, False)
            tile(3, 1, 1, False, False, True, False)
            with dve.Fori(2, T // 2 - 1) as h:
                for par in range(2):
                    tile(h * 2 + par, par, h, False, False, True, True)
            tile(T - 2, 0, T // 2 - 1, False, False, True, True)
            tile(T - 1, 1, T // 2 - 1, False, True, True, True)
            for par in range(2):
                for step in finish(T - 2 + par, T // 2 - 1, par, True):
                    step()

        @block.gpsimd
        def _(pool):
            def load_x1(t, par):
                pool.dma_start(x1[:, par, :], row(t, x1_dram)).then_inc(x1_in[par], 16)

            def tile(t, par, last):
                pool.wait_ge(t_veps, t + 1)
                nc.gpsimd.tensor_tensor(rstd[:, par:par + 1], veps[:, par:par + 1], half[:, 0:1], ALU.pow).then_inc(t_rstd, 1)
                if not last:
                    load_x1(t + 2, par)
                pool.wait_ge(y_ready, t + 1)
                pool.dma_start(row(t, y_dram), normed[:, par, :]).then_inc(y_out[par], 16)

            for par in range(2):
                load_x1(par, par)
            with pool.Fori(0, T // 2 - 1) as h:
                for par in range(2):
                    tile(h * 2 + par, par, False)
            for par in range(2):
                tile(T - 2 + par, par, True)
            for par in range(2):
                pool.wait_ge(y_out[par], 16 * (T // 2))

        @block.tensor
        def _(pe):
            def turn_group(t, par, g, first):
                pe.wait_ge(probs_ready, t * CH + g // GPC + 1)
                if not first or g >= 2:
                    pe.wait_ge(copied, t * GROUPS + g - 1)
                for k in range(PER):
                    last = nc.tensor.transpose(
                        psum[:, TURN + 2 * (g % 2) + k // (PER // 2), bass.ts(k % (PER // 2), P)],
                        E[par][:, bass.ts(g * PER + k, P)], ident[:, :])
                last.then_inc(turned, 1)

            def sum_group(t, par, g, free):
                pe.wait_ge(copied, t * GROUPS + g + 1)
                if g == 0 and free:
                    pe.wait_ge(t_y, t - 1)
                for k in range(PER):
                    last = nc.tensor.matmul(psum[:, OUT + par, 0:P], probsT[:, g % 2, bass.ts(k, P)], H[:, g * PER + k, :],
                                            start=(g == 0 and k == 0), stop=(g == GROUPS - 1 and k == PER - 1))
                last.then_inc(group_summed, 1)

            def tile(t, par, first):
                f = first and par == 0
                turn_group(t, par, 0, f)
                for g in range(GROUPS):
                    if g + 1 < GROUPS:
                        turn_group(t, par, g + 1, f)
                    sum_group(t, par, g, not first)

            tile(0, 0, True)
            tile(1, 1, True)
            with pe.Fori(1, T // 2) as h:
                for par in range(2):
                    tile(h * 2 + par, par, False)


def load_and_prepare(nc, T, mem, xn, xT, w_cheb, w_att, b, a_s, a_r, ident):
    with (
        nc.semaphore("loaded") as loaded, nc.semaphore("ones_set") as ones_set,
        nc.semaphore("prepared") as prepared,
        nc.Block() as block,
    ):
        @block.sync
        def _(sp):
            for dst, src in ((mem["nat"][:, :, :], xn), (mem["xT"][:, :], xT), (mem["w_cheb"][:, :, :], w_cheb),
                             (mem["w_att"][:, :], w_att), (mem["b_col"][:, :], b), (mem["a_s"][:, :], a_s),
                             (mem["a_r"][:, :], a_r), (mem["ident"][:, :], ident)):
                sp.dma_start(dst, src).then_inc(loaded, 16)
            sp.wait_ge(loaded, 16 * 8)

        @block.vector
        def _(dve):
            nc.vector.memset(mem["a_r_wide"][:, :], 1.0).then_inc(ones_set, 1)
            nc.vector.memset(mem["minus_half"][:, :], -0.5)
            dve.wait_ge(ones_set, 1)
            dve.wait_ge(loaded, 16 * 8)
            nc.vector.tensor_scalar(mem["a_r_wide"][:, :], mem["a_r_wide"][:, :], mem["a_r"][:, 0:1], None, ALU.mult)\
                .then_inc(prepared, 1)


def build(nc, tilesT, tiles, xn, xT, w_cheb, w_att, b, a_s, a_r, ident, y):
    T = xn.shape[1]
    x1_dram = nc.dram_tensor("x1_rows", (T, P, P), F32, kind="Internal").ap()
    shapes = {
        "nat": ([P, T, P], F32), "xT": ([P, T * P], F32), "t1T": ([P, T * P], F32), "t2T": ([P, T * P], F32),
        "ring": ([P, RING, SPAN], F32),
        "w_cheb": ([P, 3, P], F32), "w_att": ([P, P], F32), "ident": ([P, P], F32), "a_r_wide": ([P, P], F32),
        "b_col": ([P, 1], F32), "a_s": ([P, 1], F32), "a_r": ([P, 1], F32), "minus_half": ([P, 4], F32),
        "s_all": ([P, T], F32), "stats": ([P, 4, 6], F32), "mv": ([P, 4, 2], F32), "veps": ([P, 4], F32),
        "rstd": ([P, 4], F32), "mx": ([P, 2 * RING], F32), "sums": ([P, 2 * RING], F32),
        "neg_max": ([P, 2], F32), "total": ([P, 2], F32), "recip": ([P, 2], F32),
    }
    with ExitStack() as ctx:
        mem = {k: ctx.enter_context(nc.sbuf_tensor("sb_" + k, s, d)) for k, (s, d) in shapes.items()}
        mem["psum"] = ctx.enter_context(nc.psum_tensor("psum", [P, 8, BANK], F32))
        load_and_prepare(nc, T, mem, xn, xT, w_cheb, w_att, b, a_s, a_r, ident)
        diffuse(nc, "d1", tilesT, T, mem["nat"], mem, False)
        turn(nc, T, mem)
        diffuse(nc, "d2", tilesT, T, mem["nat"], mem, True)
        nodes_stage(nc, T, mem, x1_dram)
        attend(nc, T, mem, tiles, x1_dram, y)


def layouts(x, adj, L0_gnn_W, L1_gnn_W, L1_gnn_b, L1_gnn_a_s, L1_gnn_a_r):
    N = x.shape[0]
    T, S = N // P, N // SPAN
    c = np.ascontiguousarray
    return {
        "tilesT": c(adj.reshape(S, SPAN, T, P).transpose(0, 2, 3, 1)).reshape(S * T, P, SPAN),
        "tiles": c(adj.reshape(T, P, S, SPAN).transpose(0, 2, 1, 3)).reshape(T * S, P, SPAN),
        "xn": c(x.reshape(T, P, P).transpose(1, 0, 2)),
        "xT": c(x.T),
        "w_cheb": c(L0_gnn_W.transpose(2, 0, 1)),
        "w_att": c(L1_gnn_W.T),
        "b": c(L1_gnn_b.reshape(P, 1)),
        "a_s": c(L1_gnn_a_s), "a_r": c(L1_gnn_a_r),
        "ident": np.eye(P, dtype=np.float32),
    }


def kernel(x, adj, L0_gnn_W, L1_gnn_W, L1_gnn_b, L1_gnn_a_s, L1_gnn_a_r):
    import concourse.bacc as bacc
    from concourse.bass_utils import run_bass_kernel_spmd

    args = [np.asarray(a) for a in (x, adj, L0_gnn_W, L1_gnn_W, L1_gnn_b, L1_gnn_a_s, L1_gnn_a_r)]
    arrays = layouts(*args)
    N = args[0].shape[0]
    nc = bacc.Bacc("TRN2", target_bir_lowering=False, num_devices=1)
    aps = [nc.dram_tensor(k, a.shape, mybir.dt.from_np(a.dtype), kind="ExternalInput").ap() for k, a in arrays.items()]
    y = nc.dram_tensor("y", (N // P, P, P), F32, kind="ExternalOutput").ap()
    build(nc, *aps, y)
    r = run_bass_kernel_spmd(nc, [arrays], core_ids=[0])
    return r.results[0]["y"].reshape(N, P)
```

```python
from contextlib import ExitStack

import numpy as np
import concourse.bass as bass
from concourse import mybir

P = 128
BANK = 512
SPAN = 2048
RING = 4
KEPT = 8
PIECES = 4
MASKED = 2.0 ** 53
LOWEST = -3.0e38
SLOPE = 0.2
EPS = 1e-5

F32 = mybir.dt.float32
F32R = mybir.dt.float32r
ALU = mybir.AluOpType
ACT = mybir.ActivationFunctionType
AX = mybir.AxisListType


def wait_alone(engine, semaphore, value):
    engine.wait_ge(semaphore, 1)
    engine.wait_ge(semaphore, value)


def load_tile(eng, mem, tiles, n, k):
    eng.dma_start(mem["ring"][:, k, :], tiles[bass.ds(n, 1), :, :].rearrange("a p n -> (a p) n"))\
        .then_inc(mem["tile_in"][k], 16)


def diffuse(nc, name, tiles, T, mem, second):
    SUP = T * P // SPAN
    QUADS = T // RING
    BANKS = SPAN // BANK
    ring, psum, kept, nodes = mem["ring"], mem["psum"], mem["kept"], mem["nat"]
    tile_in, kept_in, nat_in = mem["tile_in"], mem["kept_in"], mem["nat_in"]
    out = mem["t2T" if second else "t1T"]
    before = (SUP * QUADS - KEPT // RING) if second else 0
    PP = QUADS // PIECES
    if second:
        GROUP, AT_ONCE = QUADS // 4, KEPT // 4
        RUNS = [run for g in range(4) for run in ((g * GROUP, (g + 1) * GROUP - 1, g * AT_ONCE, 0),
                                                  ((g + 1) * GROUP - 1, (g + 1) * GROUP, g * AT_ONCE, AT_ONCE))]
    else:
        RUNS = [(q, q + 1, q * RING, RING) for q in range(KEPT // RING)] + [(KEPT // RING, PP, KEPT, 0)] \
            + [(p * PP, (p + 1) * PP, KEPT, 0) for p in range(1, PIECES)]
    assert SUP % 2 == 0 and KEPT % RING == 0 and KEPT // RING < PP

    def first_span(engine, step, before_run=None):
        def quad(place, used, at_end):
            for j in range(RING):
                here = j - (RING - at_end)
                step(place, j, used + here if here >= 0 else None, used)

        for lo, hi, used, at_end in RUNS:
            if before_run:
                before_run(lo)
            if lo == 0 or at_end:
                quad(lo, used, at_end)
                lo += 1
            if lo < hi:
                with engine.Fori(lo, hi) as place:
                    quad(place, used, 0)

    def later_quads(engine, step, lo, hi):
        with engine.Fori(lo, hi) as place:
            for j in range(RING):
                step(place, j, None, KEPT)

    def source(j, kept_number, used):
        return ring[:, (j - used) % RING, :] if kept_number is None else kept[kept_number]

    with ExitStack() as ctx:
        def sem(what):
            return ctx.enter_context(nc.semaphore(f"{name}_{what}"))

        def sbuf(what, shape, dtype):
            return ctx.enter_context(nc.sbuf_tensor(f"{name}_{what}", shape, dtype))

        high = sbuf("high", [P, 2, SPAN], F32R)
        low = sbuf("low", [P, 2, SPAN], F32R)
        w_high = sbuf("w_high", [P, RING, P], F32R)
        w_low = sbuf("w_low", [P, RING, P], F32R)
        w_full = sbuf("w_full", [P, RING, P], F32)
        high_ready = sem("high_ready")
        low_ready = sem("low_ready")
        w_copied = sem("w_copied")
        w_ready = sem("w_ready")
        high_summed = sem("high_summed")
        tile_summed = sem("tile_summed")
        bank_free = sem("bank_free")
        block = ctx.enter_context(nc.Block())

        @block.sync
        def _(sp):
            def refill(place, j, kept_number, used):
                if kept_number is None:
                    sp.wait_ge(low_ready, place * RING + (j + 1))
                    load_tile(sp, mem, tiles, place * RING + (j - used + RING + KEPT), (j - used) % RING)

            first_span(sp, refill)
            later_quads(sp, refill, QUADS, SUP * QUADS - 1)
            if second:
                for p, loaded in enumerate(mem["xT_in"]):
                    sp.dma_start(mem["xT"][:, bass.ts(p, SPAN)], mem["xT_dram"][:, bass.ts(p, SPAN)]).then_inc(loaded, 16)

        @block.gpsimd
        def _(pool):
            def split(n, node, k):
                if not isinstance(n, int) or n >= RING:
                    pool.wait_ge(tile_summed, n - (RING - 1))
                src = nodes[:, bass.ds(node, 1), :].rearrange("p a d -> p (a d)")
                nc.gpsimd.tensor_copy(w_full[:, k, :], src).then_inc(w_copied, 1)
                nc.gpsimd.tensor_copy(w_high[:, k, :], src).then_inc(w_copied, 1)
                pool.wait_ge(w_copied, 2 * n + 2)
                nc.gpsimd.tensor_tensor(w_low[:, k, :], w_full[:, k, :], w_high[:, k, :].bitcast(F32), ALU.subtract)\
                    .then_inc(w_ready, 1)

            def step(place, j, kept_number, used):
                n = place * RING + j
                split(n, n + (KEPT - used) if kept_number is None else kept_number, j)

            def nodes_loaded(place):
                if not second and place % PP == 0:
                    pool.wait_ge(nat_in[place // PP], 16)

            first_span(pool, step, nodes_loaded)
            with pool.Fori(1, SUP) as s:
                with pool.Fori(0, QUADS) as q:
                    for k in range(RING):
                        split((s * QUADS + q) * RING + k, q * RING + k, k)

        @block.scalar
        def _(act):
            def split(place, j, kept_number, used):
                n = place * RING + j
                if kept_number is None:
                    act.wait_ge(tile_in[(j - used) % RING], (place + (j - used) // RING) * 16 + 16 * (before + 1))
                elif not second:
                    act.wait_ge(kept_in[kept_number], 16)
                if not isinstance(n, int) or n >= 2:
                    act.wait_ge(high_summed, n - 1)
                    act.wait_ge(low_ready, n - 1)
                nc.scalar.activation(high[:, j % 2, :], source(j, kept_number, used), ACT.Copy).then_inc(high_ready, 1)

            first_span(act, split)
            later_quads(act, split, QUADS, SUP * QUADS)

        @block.vector
        def _(dve):
            def split(place, j, kept_number, used):
                n = place * RING + j
                dve.wait_ge(high_ready, n + 1)
                if not isinstance(n, int) or n >= 2:
                    dve.wait_ge(tile_summed, n - 1)
                nc.vector.tensor_tensor(low[:, j % 2, :], source(j, kept_number, used), high[:, j % 2, :].bitcast(F32),
                                        ALU.subtract).then_inc(low_ready, 1)

            def drain(s, par, b):
                dve.wait_ge(tile_summed, s * (QUADS * RING) + QUADS * RING)
                nc.vector.tensor_copy(out[:, bass.ds(s * SPAN + b * BANK, BANK)], psum[:, par * BANKS + b, :]).then_inc(bank_free, 1)

            def later_span(s, par):
                for j in range(RING):
                    split(s * QUADS, j, None, KEPT)
                    for b in ((), (0,), (1,), (2, 3))[j]:
                        drain(s - 1, 1 - par, b)
                later_quads(dve, split, s * QUADS + 1, s * QUADS + QUADS)

            first_span(dve, split)
            later_span(1, 1)
            with dve.Fori(1, SUP // 2) as h:
                for par in range(2):
                    later_span(h * 2 + par, par)
            for b in range(BANKS):
                drain(SUP - 1, 1, b)

        @block.tensor
        def _(pe):
            def tile(s, par, q, k, start, stop, first):
                n = (s * QUADS + q) * RING + k
                banks = range(par * BANKS, (par + 1) * BANKS)
                pe.wait_ge(w_ready, n + 1)
                pe.wait_ge(high_ready, n + 1)
                for b, bank in enumerate(banks):
                    if start and not first:
                        pe.wait_ge(bank_free, s * BANKS + (b + 1 - 2 * BANKS))
                    nc.tensor.matmul(psum[:, bank, :], w_high[:, k, :], high[:, k % 2, bass.ts(b, BANK)], start=start, stop=False)
                for b, bank in enumerate(banks):
                    last = nc.tensor.matmul(psum[:, bank, :], w_low[:, k, :], high[:, k % 2, bass.ts(b, BANK)],
                                            start=False, stop=False)
                last.then_inc(high_summed, 1)
                pe.wait_ge(low_ready, n + 1)
                for b, bank in enumerate(banks):
                    last = nc.tensor.matmul(psum[:, bank, :], w_high[:, k, :], low[:, k % 2, bass.ts(b, BANK)],
                                            start=False, stop=stop)
                last.then_inc(tile_summed, 1)

            def span(s, par, first):
                for k in range(RING):
                    tile(s, par, 0, k, k == 0, False, first)
                with pe.Fori(1, QUADS - 1) as q:
                    for k in range(RING):
                        tile(s, par, q, k, False, False, False)
                for k in range(RING):
                    tile(s, par, QUADS - 1, k, False, k == RING - 1, False)

            span(0, 0, True)
            span(1, 1, True)
            with pe.Fori(1, SUP // 2) as h:
                for par in range(2):
                    span(h * 2 + par, par, False)


def turn(nc, T, mem, tiles):
    t1T, nat, ident, psum = mem["t1T"], mem["nat"], mem["ident"], mem["psum"]
    PER = BANK // P
    GROUPS = T // PER
    with (
        nc.semaphore("turned") as turned,
        nc.semaphore("turn_copied0") as copied0,
        nc.semaphore("turn_copied1") as copied1,
        nc.Block() as block,
    ):
        copied = [copied0, copied1]

        @block.sync
        def _(sp):
            for k in range(RING):
                load_tile(sp, mem, tiles, KEPT + k, k)

        @block.tensor
        def _(pe):
            for g in range(GROUPS):
                if g >= 8:
                    pe.wait_ge(copied[g % 2], (g - 8) // 2 + 1)
                for k in range(PER):
                    last = nc.tensor.transpose(psum[:, g % 8, bass.ts(k, P)], t1T[:, bass.ts(g * PER + k, P)], ident[:, :])
                last.then_inc(turned, 1)

        def rows(g):
            return nat[:, bass.ts(g, PER), :].rearrange("p a d -> p (a d)")

        @block.vector
        def _(dve):
            for g in range(0, GROUPS, 2):
                dve.wait_ge(turned, g + 1)
                nc.vector.tensor_copy(rows(g), psum[:, g % 8, :]).then_inc(copied[0], 1)

        @block.scalar
        def _(act):
            for g in range(1, GROUPS, 2):
                act.wait_ge(turned, g + 1)
                nc.scalar.activation(rows(g), psum[:, g % 8, :], ACT.Copy).then_inc(copied[1], 1)


def nodes_stage(nc, T, mem, x1_dram, chunks):
    xT, t1T, t2T, nat, psum, ident = (mem[k] for k in ("xT", "t1T", "t2T", "nat", "psum", "ident"))
    w_cheb, w_att, w_r, b_rows, s_bias, r_bias = (mem[k] for k in ("w_cheb", "w_att", "w_r", "b_rows", "s_bias", "r_bias"))
    s_all, half = mem["s_all"], mem["minus_half"]
    PER = BANK // P
    CH = T // PER
    stats, mv, rstd, veps = mem["stats"], mem["mv"], mem["rstd"], mem["veps"]
    COMBO, Y, X1T, RB, HN = (0, 7), 1, 3, 4, 5
    with ExitStack() as ctx:
        def sem(name):
            return ctx.enter_context(nc.semaphore(name))

        def sbuf(name, shape):
            return ctx.enter_context(nc.sbuf_tensor(name, shape, F32))

        yT = sbuf("yT", [P, 2, BANK])
        x1T = sbuf("x1T", [P, 2, BANK])
        x1 = sbuf("x1", [P, 2, BANK])
        xT_in = mem["xT_in"]
        t2_ready = sem("t2_ready")
        combo_done = sem("combo_done")
        yT_ready = sem("yT_ready")
        y_turned = sem("y_turned")
        n_stats = sem("n_stats")
        n_mv = sem("n_mv")
        n_veps = sem("n_veps")
        n_rstd = sem("n_rstd")
        x1_ready = sem("x1_ready")
        x1_turned = sem("x1_turned")
        x1T_ready = sem("x1T_ready")
        proj_done = sem("proj_done")
        r_kept = sem("r_kept")
        h_kept = sem("h_kept")
        stored = [sem(f"x1_stored{k}") for k in range(2)]
        block = ctx.enter_context(nc.Block())

        @block.tensor
        def _(pe):
            def combine(c):
                if c == 0:
                    pe.wait_ge(mem["w_cheb_in"], 16)
                pe.wait_ge(t2_ready, c + 1)
                if c >= 2:
                    pe.wait_ge(yT_ready, c - 1)
                for j, src in enumerate((xT, t1T, t2T)):
                    last = nc.tensor.matmul(psum[:, COMBO[c % 2], :], w_cheb[:, j, :], src[:, bass.ts(c, BANK)],
                                            start=j == 0, stop=j == 2)
                last.then_inc(combo_done, 1)

            def turn_y(c):
                pe.wait_ge(yT_ready, c + 1)
                if c >= 2:
                    pe.wait_ge(x1_ready, c - 1)
                for k in range(PER):
                    last = nc.tensor.transpose(psum[:, Y + c % 2, bass.ts(k, P)], yT[:, c % 2, bass.ts(k, P)], ident[:, :])
                last.then_inc(y_turned, 1)

            def turn_x1(c):
                pe.wait_ge(x1_ready, c + 1)
                if c >= 1:
                    pe.wait_ge(x1T_ready, c)
                for k in range(PER):
                    last = nc.tensor.transpose(psum[:, X1T, bass.ts(k, P)], x1[:, c % 2, bass.ts(k, P)], ident[:, :])
                last.then_inc(x1_turned, 1)

            def project(c):
                pe.wait_ge(x1T_ready, c + 1)
                if c >= 1:
                    pe.wait_ge(r_kept, c)
                    pe.wait_ge(h_kept, c)
                nc.tensor.matmul(psum[:, RB, :], w_r[:, :], x1T[:, c % 2, :], start=True, stop=True)
                for k in range(PER):
                    last = nc.tensor.matmul(psum[:, HN + k // 2, bass.ts(k % 2, P + 1)], x1T[:, c % 2, bass.ts(k, P)],
                                            w_att[:, :], start=True, stop=True)
                last.then_inc(proj_done, 1)

            for i in range(CH + 4):
                for lag, step in ((0, combine), (1, turn_y), (3, turn_x1), (4, project)):
                    if 0 <= i - lag < CH:
                        step(i - lag)

        @block.vector
        def _(dve):
            def t2(c):
                cols = bass.ts(c, BANK)
                dve.wait_ge(xT_in[c * BANK // SPAN], 16)
                nc.vector.scalar_tensor_tensor(t2T[:, cols], t2T[:, cols], 2.0, xT[:, cols], ALU.mult, ALU.subtract)\
                    .then_inc(t2_ready, 1)

            def residual(c):
                dve.wait_ge(combo_done, c + 1)
                if c >= 2:
                    dve.wait_ge(y_turned, c - 1)
                nc.vector.tensor_tensor(yT[:, c % 2, :], psum[:, COMBO[c % 2], :], xT[:, bass.ts(c, BANK)], ALU.add)\
                    .then_inc(yT_ready, 1)

            def rows(c):
                return psum[:, Y + c % 2, :].rearrange("p (a n) -> p a n", a=PER)

            def moments(c):
                dve.wait_ge(y_turned, c + 1)
                for k in range(PER):
                    nc.vector.bn_stats(stats[:, k, :], rows(c)[:, k, :]).then_inc(n_stats, 1)
                if c >= 1:
                    dve.wait_ge(x1_ready, c)
                dve.wait_ge(n_stats, PER * (c + 1))
                for k in range(PER):
                    nc.vector.bn_aggr(mv[:, k, :], stats[:, k, :]).then_inc(n_mv, 1)

            def norm(c):
                dve.wait_ge(n_rstd, c + 1)
                if c >= 2:
                    dve.wait_ge(stored[c % 2], 16 * (c // 2))
                    dve.wait_ge(x1_turned, c - 1)
                for k in range(PER):
                    last = nc.vector.tensor_scalar(x1[:, c % 2, bass.ts(k, P)], rows(c)[:, k, :], mv[:, k, 0:1],
                                                   rstd[:, k:k + 1], ALU.subtract, ALU.mult)
                last.then_inc(x1_ready, 1)

            def keep_h(c):
                dve.wait_ge(proj_done, c + 1)
                hs = psum[:, HN:HN + 2, 0:2 * (P + 1)].rearrange("p a (b n) -> p a b n", b=2)
                nc.vector.tensor_tensor(nat[:, bass.ts(c, PER), :].rearrange("p (a b) d -> p a b d", a=2), hs[:, :, :, 0:P],
                                        b_rows[:, :, :, :], ALU.add)
                nc.vector.tensor_scalar(s_all[:, bass.ts(c, PER)].rearrange("p (a b) -> p a b", a=2), hs[:, :, :, P],
                                        s_bias[:, 0:1], -1.0 / MASKED, ALU.add, ALU.mult).then_inc(h_kept, 1)

            t2(0)
            for i in range(CH + 5):
                for lag, step in ((2, moments), (-1, t2), (5, keep_h), (0, residual), (2, norm)):
                    if 0 <= i - lag < CH and (step is not t2 or i - lag > 0):
                        step(i - lag)

        @block.gpsimd
        def _(pool):
            for c in range(CH):
                pool.wait_ge(n_mv, PER * (c + 1))
                nc.gpsimd.tensor_scalar(veps[:, 0:PER], mv[:, 0:PER, 1], EPS, None, ALU.add).then_inc(n_veps, 1)
                pool.wait_ge(n_veps, c + 1)
                nc.gpsimd.tensor_tensor(rstd[:, 0:PER], veps[:, 0:PER], half[:, 0:PER], ALU.pow).then_inc(n_rstd, 1)

        @block.scalar
        def _(act):
            def keep_x1T(c):
                act.wait_ge(x1_turned, c + 1)
                if c >= 2:
                    act.wait_ge(proj_done, c - 1)
                nc.scalar.activation(x1T[:, c % 2, :], psum[:, X1T, :], ACT.Copy).then_inc(x1T_ready, 1)

            def keep_r(c):
                act.wait_ge(proj_done, c + 1)
                nc.scalar.activation(xT[:, bass.ts(c, BANK)], psum[:, RB, :], ACT.Identity, bias=r_bias[:, 0:1],
                                     scale=-1.0 / MASKED).then_inc(r_kept, 1)

            for i in range(CH + 4):
                for lag, step in ((3, keep_x1T), (4, keep_r)):
                    if 0 <= i - lag < CH:
                        step(i - lag)

        @block.sync
        def _(sp):
            for k in range(RING):
                load_tile(sp, mem, chunks, k, k)
            for c in range(CH):
                sp.wait_ge(x1_ready, c + 1)
                sp.dma_start(x1_dram[bass.ts(c, PER), :, :].rearrange("a p d -> p a d"),
                             x1[:, c % 2, :].rearrange("p (a d) -> p a d", a=PER)).then_inc(stored[c % 2], 16)
            for k in range(2):
                sp.wait_ge(stored[k], 16 * ((CH + 1 - k) // 2))


def attend(nc, T, mem, chunks, x1_dram, y_dram):
    R, H, psum, ident, ring = mem["xT"], mem["nat"], mem["psum"], mem["ident"], mem["ring"]
    E = [mem["t1T"], mem["t2T"]]
    s_all, half, eps, zero, minus_mean, shift = (mem[k] for k in ("s_all", "minus_half", "eps", "zero", "minus_mean", "shift"))
    CH = T * P // SPAN
    assert CH == RING
    chunk_in, before = mem["tile_in"], 2 * (T * P // SPAN * (T // RING) - KEPT // RING)
    GW = 2 * BANK
    GROUPS = T * P // GW
    GPC = SPAN // GW
    PER = GW // P
    mx, neg_max, sums = mem["mx"], mem["neg_max"], mem["sums"]
    total, recip, stats, mv, veps, rstd = (mem[k] for k in ("total", "recip", "stats", "mv", "veps", "rstd"))
    TURN, OUT = 0, 4
    with ExitStack() as ctx:
        def sem(name):
            return ctx.enter_context(nc.semaphore(name))

        def sbuf(name, shape):
            return ctx.enter_context(nc.sbuf_tensor("a_" + name, shape, F32))

        rest = sbuf("rest", [P, 2, SPAN])
        probsT = sbuf("probsT", [P, 2, GW])
        x1, y, normed = sbuf("x1", [P, 2, P]), sbuf("y", [P, 2, P]), sbuf("normed", [P, 2, P])

        products = sem("a_products")
        scored = sem("a_scored")
        slopes = sem("a_slopes")
        rests = sem("a_rests")
        max_ready = sem("a_max_ready")
        probs_ready = sem("a_probs_ready")
        turned = sem("a_turned")
        copied = sem("a_copied")
        group_summed = sem("a_group_summed")
        t_total = sem("a_t_total")
        t_recip = sem("a_t_recip")
        t_y = sem("a_t_y")
        t_stats = sem("a_t_stats")
        t_mv = sem("a_t_mv")
        t_veps = sem("a_t_veps")
        t_scaled = sem("a_t_scaled")
        t_shift = sem("a_t_shift")
        t_rstd = sem("a_t_rstd")
        y_ready = sem("a_y_ready")
        x1_in = [sem(f"a_x1_in{p}") for p in range(2)]
        y_out = [sem(f"a_y_out{p}") for p in range(2)]
        block = ctx.enter_context(nc.Block())

        def row(t, dram):
            return dram[bass.ds(t, 1), :, :].rearrange("a p d -> (a p) d")

        @block.sync
        def _(sp):
            with sp.Fori(1, T) as t:
                for c in range(CH):
                    sp.wait_ge(rests, (t - 1) * CH + c + 1)
                    load_tile(sp, mem, chunks, t * CH + c, c)

        @block.scalar
        def _(act):
            def slope(t, par, c, first):
                act.wait_ge(products, t * CH + c + 1)
                if not first or c >= 2:
                    act.wait_ge(scored, t * CH + c - 1)
                nc.scalar.activation(rest[:, c % 2, :], E[par][:, bass.ts(c, SPAN)], ACT.Relu, scale=1.0 - SLOPE)\
                    .then_inc(slopes, 1)

            def exps(t, par, c):
                if c == 0:
                    act.wait_ge(max_ready, t + 1)
                e = E[par][:, bass.ts(c, SPAN)]
                nc.scalar.activation(e, e, ACT.Exp, bias=neg_max[:, par:par + 1],
                                     accum_out=sums[:, par * RING + c:par * RING + c + 1]).then_inc(probs_ready, 1)

            def copy(t, g, first):
                act.wait_ge(turned, t * GROUPS + g + 1)
                if not first or g >= 2:
                    act.wait_ge(group_summed, t * GROUPS + g - 1)
                nc.scalar.activation(probsT[:, g % 2, :],
                                     psum[:, TURN + 2 * (g % 2):TURN + 2 * (g % 2) + 2, :].rearrange("p a n -> p (a n)"),
                                     ACT.Copy).then_inc(copied, 1)

            def scale_output(t, par):
                act.wait_ge(group_summed, (t + 1) * GROUPS)
                act.wait_ge(t_recip, t + 1)
                nc.scalar.activation(y[:, par, :], psum[:, OUT + par, 0:P], ACT.Copy, scale=recip[:, par:par + 1])\
                    .then_inc(t_scaled, 1)

            def norm(t, u, par):
                act.wait_ge(t_shift, t + 1)
                if not isinstance(u, int) or u > 0:
                    act.wait_ge(y_out[par], 16 * u)
                nc.scalar.activation(normed[:, par, :], y[:, par, :], ACT.Identity, bias=shift[:, par:par + 1],
                                     scale=rstd[:, par:par + 1]).then_inc(y_ready, 1)

            def tile(t, par, first, ahead, u=0):
                for c in range(CH):
                    if ahead:
                        slope(t + 1, 1 - par, c, False)
                    exps(t, par, c)
                    if c:
                        for g in range(GPC * (c - 1), GPC * c):
                            copy(t, g, first and par == 0)
                    elif not first or par:
                        for g in range(GPC * (CH - 1), GROUPS):
                            copy(t - 1, g, False)
                    if c == CH - 1:
                        if not first:
                            norm(t - 2, u - 1, par)
                        if not first or par:
                            scale_output(t - 1, 1 - par)

            for c in range(CH):
                slope(0, 0, c, True)
            tile(0, 0, True, True)
            tile(1, 1, True, True)
            for par in range(2):
                tile(2 + par, par, False, True, 1)
            with act.Fori(2, T // 2 - 1) as h:
                for par in range(2):
                    tile(h * 2 + par, par, False, True, h)
            tile(T - 2, 0, False, True, T // 2 - 1)
            tile(T - 1, 1, False, False, T // 2 - 1)
            for g in range(GPC * (CH - 1), GROUPS):
                copy(T - 1, g, False)
            norm(T - 2, T // 2 - 1, 0)
            scale_output(T - 1, 1)
            norm(T - 1, T // 2 - 1, 1)

        @block.vector
        def _(dve):
            def product(t, par, c, first):
                n = t * CH + c
                dve.wait_ge(chunk_in[c], 16 * t + 16 * (before + 1))
                if not first:
                    dve.wait_ge(turned, (t - 2) * GROUPS + GPC * (c + 1))
                nc.vector.scalar_tensor_tensor(E[par][:, bass.ts(c, SPAN)], R[:, bass.ts(c, SPAN)], s_all[:, bass.ds(t, 1)],
                                               ring[:, c, :], ALU.add, ALU.mult).then_inc(products, 1)

            def mask(t, c):
                dve.wait_ge(slopes, t * CH + c + 1)
                nc.vector.scalar_tensor_tensor(rest[:, c % 2, :], ring[:, c, :], 0.0, rest[:, c % 2, :],
                                               ALU.is_le, ALU.subtract).then_inc(rests, 1)

            def score(t, par, c):
                e = E[par][:, bass.ts(c, SPAN)]
                wait_alone(dve, rests, t * CH + c + 1)
                nc.vector.tensor_tensor_reduce(e, e, rest[:, c % 2, :], -MASKED, LOWEST, ALU.add, ALU.max,
                                               accum_out=mx[:, par * RING + c:par * RING + c + 1]).then_inc(scored, 1)

            def maximum(t, par, first):
                dve.wait_ge(scored, t * CH + CH)
                if not first:
                    dve.wait_ge(probs_ready, (t - 1) * CH)
                nc.vector.tensor_reduce(neg_max[:, par:par + 1], mx[:, par * RING:par * RING + CH], AX.X, ALU.max,
                                        negate=True).then_inc(max_ready, 1)

            def total_steps(t, par, free):
                one = slice(par, par + 1)

                def add_totals():
                    dve.wait_ge(probs_ready, (t + 1) * CH)
                    nc.vector.reduce_sum(total[:, one], sums[:, par * RING:par * RING + CH], AX.X).then_inc(t_total, 1)

                def invert():
                    dve.wait_ge(t_total, t + 1)
                    if free:
                        dve.wait_ge(t_scaled, t - 1)
                    nc.vector.reciprocal(recip[:, one], total[:, one]).then_inc(t_recip, 1)

                return [add_totals, invert]

            def moment_steps(t, par):
                def moments():
                    dve.wait_ge(t_y, t + 1)
                    nc.vector.bn_stats(stats[:, par, :], y[:, par, :]).then_inc(t_stats, 1)

                def mean_and_variance():
                    wait_alone(dve, t_stats, t + 1)
                    nc.vector.bn_aggr(mv[:, par, :], stats[:, par, :]).then_inc(t_mv, 1)

                return [moments, mean_and_variance]

            def tile(t, par, first, last, number=None):
                steps = []
                if number is None or number >= 2:
                    steps += total_steps(t - 2, par, number is None or number >= 4)
                if number is None or number >= 3:
                    steps += moment_steps(t - 3, 1 - par)
                slot = 0
                for c in range(CH):
                    for work in (mask, product, score):
                        if work is mask:
                            mask(t, c)
                        elif work is score:
                            score(t, par, c)
                        elif c + 2 < CH:
                            product(t, par, c + 2, first)
                        elif not last:
                            product(t + 1, 1 - par, c + 2 - CH, first and par == 0)
                        slot += 1
                        if steps and slot >= 3:
                            steps.pop(0)()
                maximum(t, par, first)

            MID = 4 + (T - 6) % 4
            for c in range(2):
                product(0, 0, c, True)
            tile(0, 0, True, False, 0)
            tile(1, 1, True, False, 1)
            tile(2, 0, False, False, 2)
            tile(3, 1, False, False, 3)
            for t in range(4, MID):
                tile(t, t % 2, False, False)
            with dve.Fori(0, (T - 2 - MID) // 4) as h:
                for k in range(4):
                    tile(h * 4 + (MID + k), (MID + k) % 2, False, False)
            tile(T - 2, 0, False, False)
            tile(T - 1, 1, False, True)
            for steps in (total_steps(T - 2, 0, True), moment_steps(T - 3, 1), total_steps(T - 1, 1, True),
                          moment_steps(T - 2, 0), moment_steps(T - 1, 1)):
                for step in steps:
                    step()

        @block.gpsimd
        def _(pool):
            def load_x1(t, par):
                pool.dma_start(x1[:, par, :], row(t, x1_dram)).then_inc(x1_in[par], 16)

            def add_x1(t, u, par, last):
                pool.wait_ge(t_scaled, t + 1)
                pool.wait_ge(x1_in[par], 16 * u + 16)
                nc.gpsimd.tensor_tensor(y[:, par, :], y[:, par, :], x1[:, par, :], ALU.add).then_inc(t_y, 1)
                if not last:
                    pool.wait_ge(t_y, t + 1)
                    load_x1(t + 2, par)

            def scale_and_shift(t, par):
                one = slice(par, par + 1)
                pool.wait_ge(t_mv, t + 1)
                nc.gpsimd.tensor_tensor(veps[:, one], mv[:, par, 1:2], eps[:, :], ALU.add)
                nc.gpsimd.tensor_tensor(minus_mean[:, one], zero[:, :], mv[:, par, 0:1], ALU.subtract).then_inc(t_veps, 1)
                pool.wait_ge(t_veps, t + 1)
                nc.gpsimd.tensor_tensor(rstd[:, one], veps[:, one], half[:, 0:1], ALU.pow).then_inc(t_rstd, 1)
                pool.wait_ge(t_rstd, t + 1)
                nc.gpsimd.tensor_tensor(shift[:, one], minus_mean[:, one], rstd[:, one], ALU.mult).then_inc(t_shift, 1)

            def store(t, par):
                pool.wait_ge(y_ready, t + 1)
                pool.dma_start(row(t, y_dram), normed[:, par, :]).then_inc(y_out[par], 16)

            def tile(t, u, par, first, last):
                if not first:
                    scale_and_shift(t - 1, 1 - par)
                    store(t - 1, 1 - par)
                add_x1(t, u, par, last)

            for par in range(2):
                load_x1(par, par)
            tile(0, 0, 0, True, False)
            tile(1, 0, 1, False, False)
            with pool.Fori(1, T // 2 - 1) as h:
                for par in range(2):
                    tile(h * 2 + par, h, par, False, False)
            for par in range(2):
                tile(T - 2 + par, T // 2 - 1, par, False, True)
            scale_and_shift(T - 1, 1)
            store(T - 1, 1)
            for par in range(2):
                pool.wait_ge(y_out[par], 16 * (T // 2))

        @block.tensor
        def _(pe):
            def turn_group(t, par, g, first):
                pe.wait_ge(probs_ready, t * CH + g // GPC + 1)
                if not first or g >= 2:
                    pe.wait_ge(copied, t * GROUPS + g - 1)
                for k in range(PER):
                    last = nc.tensor.transpose(
                        psum[:, TURN + 2 * (g % 2) + k // (PER // 2), bass.ts(k % (PER // 2), P)],
                        E[par][:, bass.ts(g * PER + k, P)], ident[:, :])
                last.then_inc(turned, 1)

            def sum_group(t, par, g, free):
                pe.wait_ge(copied, t * GROUPS + g + 1)
                if g == 0 and free:
                    pe.wait_ge(t_scaled, t - 1)
                for k in range(PER):
                    last = nc.tensor.matmul(psum[:, OUT + par, 0:P], probsT[:, g % 2, bass.ts(k, P)], H[:, g * PER + k, :],
                                            start=(g == 0 and k == 0), stop=(g == GROUPS - 1 and k == PER - 1))
                last.then_inc(group_summed, 1)

            def tile(t, par, first):
                f = first and par == 0
                turn_group(t, par, 0, f)
                for g in range(GROUPS):
                    if g + 1 < GROUPS:
                        turn_group(t, par, g + 1, f)
                    sum_group(t, par, g, not first)

            tile(0, 0, True)
            tile(1, 1, True)
            with pe.Fori(1, T // 2) as h:
                for par in range(2):
                    tile(h * 2 + par, par, False)


def load_and_prepare(nc, T, mem, tiles, dram):
    nat, kept, psum = mem["nat"], mem["kept"], mem["psum"]
    w_att, w_r, a_r_wide, ones, b_rhs = (mem[k] for k in ("w_att", "w_r", "a_r_wide", "ones", "b_rhs"))
    small = ("w_att_rows", "ident", "a_r", "a_s", "b_col")
    with ExitStack() as ctx:
        def sem(name):
            return ctx.enter_context(nc.semaphore(name))

        loaded, set_, operands, products, prepared = (sem(n) for n in ("loaded", "ones_set", "operands", "w_products", "prepared"))
        block = ctx.enter_context(nc.Block())

        @block.scalar
        def _(act):
            act.dma_start(mem["w_cheb"][:], dram["w_cheb"]).then_inc(mem["w_cheb_in"], 16)

        @block.sync
        def _(sp):
            for name in small:
                sp.dma_start(mem[name][:], dram[name]).then_inc(loaded, 16)
            sp.dma_start(w_att[:, 0:P], dram["w_att"]).then_inc(loaded, 16)
            per = T // PIECES
            for piece in range(PIECES):
                sp.dma_start(nat[:, bass.ts(piece, per), :], dram["xn"][:, bass.ts(piece, per), :]).then_inc(mem["nat_in"][piece], 16)
                for n in range(piece * KEPT // PIECES, (piece + 1) * KEPT // PIECES):
                    sp.dma_start(kept[n], tiles[n, :, :]).then_inc(mem["kept_in"][n], 16)
            for k in range(RING):
                load_tile(sp, mem, tiles, KEPT + k, k)

        @block.vector
        def _(dve):
            nc.vector.memset(ones[:, :], 1.0).then_inc(set_, 1)
            for name, value in (("minus_half", -0.5), ("eps", EPS), ("zero", 0.0)):
                nc.vector.memset(mem[name][:, :], value)
            dve.wait_ge(set_, 1)
            dve.wait_ge(loaded, 16 * (len(small) + 1))
            b = mem["b_col"][:, 0:1]
            nc.vector.tensor_scalar(a_r_wide[:, :], ones[:, :], mem["a_r"][:, 0:1], None, ALU.mult)
            nc.vector.tensor_scalar(b_rhs[:, 0:P], mem["ident"][:, :], b, None, ALU.mult)
            nc.vector.tensor_scalar(b_rhs[:, P:P + 1], mem["a_s"][:, :], b, None, ALU.mult)
            nc.vector.tensor_scalar(b_rhs[:, P + 1:P + 2], mem["a_r"][:, :], b, None, ALU.mult).then_inc(operands, 1)
            dve.wait_ge(products, 1)
            nc.vector.tensor_copy(w_r[:, :], psum[:, 0, 0:P])
            nc.vector.tensor_copy(w_att[:, P:P + 1], psum[:, 1, 0:1])
            for k in range(4):
                nc.vector.tensor_copy(mem["b_rows"][:, k // 2, k % 2, :], psum[:, 2, 0:P])
            nc.vector.tensor_copy(mem["s_bias"][:, :], psum[:, 2, P:P + 1])
            nc.vector.tensor_scalar(mem["r_bias"][:, :], psum[:, 2, P + 1:P + 2], -1.0 / MASKED, None, ALU.mult)\
                .then_inc(prepared, 1)

        @block.tensor
        def _(pe):
            pe.wait_ge(operands, 1)
            rows = mem["w_att_rows"]
            nc.tensor.matmul(psum[:, 0, 0:P], rows[:, :], a_r_wide[:, :], start=True, stop=True)
            nc.tensor.matmul(psum[:, 1, 0:1], rows[:, :], mem["a_s"][:, :], start=True, stop=True)
            nc.tensor.matmul(psum[:, 2, 0:P + 2], ones[:, :], b_rhs[:, :], start=True, stop=True).then_inc(products, 1)


def build(nc, dram, y):
    T = dram["xn"].shape[1]
    x1_dram = nc.dram_tensor("x1_rows", (T, P, P), F32, kind="Internal").ap()
    shapes = {
        "nat": ([P, T, P]), "xT": ([P, T * P]), "t1T": ([P, T * P]), "t2T": ([P, T * P]),
        "ring": ([P, RING, SPAN]),
        "w_cheb": ([P, 3, P]), "w_att": ([P, P + 1]), "w_att_rows": ([P, P]), "w_r": ([P, P]), "a_r_wide": ([P, P]),
        "ones": ([P, P]), "ident": ([P, P]), "b_rhs": ([P, P + 2]), "b_rows": ([P, 2, 2, P]),
        "b_col": ([P, 1]), "a_s": ([P, 1]), "a_r": ([P, 1]), "s_bias": ([P, 1]), "r_bias": ([P, 1]), "minus_half": ([P, 4]),
        "eps": ([P, 1]), "zero": ([P, 1]), "minus_mean": ([P, 2]), "shift": ([P, 2]),
        "s_all": ([P, T]), "stats": ([P, 4, 6]), "mv": ([P, 4, 2]), "veps": ([P, 4]),
        "rstd": ([P, 4]), "mx": ([P, 2 * RING]), "sums": ([P, 2 * RING]),
        "neg_max": ([P, 2]), "total": ([P, 2]), "recip": ([P, 2]),
    }
    with ExitStack() as ctx:
        def sems(name, n):
            return [ctx.enter_context(nc.semaphore(f"{name}{k}")) for k in range(n)]

        mem = {k: ctx.enter_context(nc.sbuf_tensor("sb_" + k, s, F32)) for k, s in shapes.items()}
        mem["psum"] = ctx.enter_context(nc.psum_tensor("psum", [P, 8, BANK], F32))
        mem["tile_in"], mem["kept_in"], mem["nat_in"] = sems("tile_in", RING), sems("kept_in", KEPT), sems("nat_in", PIECES)
        mem["w_cheb_in"] = ctx.enter_context(nc.semaphore("w_cheb_in"))
        mem["xT_in"], mem["xT_dram"] = sems("xT_in", T * P // SPAN), dram["xT"]
        mem["kept"] = [mem[("t2T", "xT")[n // (KEPT // 2)]][:, bass.ts(n % (KEPT // 2), SPAN)] for n in range(KEPT)]
        load_and_prepare(nc, T, mem, dram["tilesT"], dram)
        diffuse(nc, "d1", dram["tilesT"], T, mem, False)
        turn(nc, T, mem, dram["tilesT"])
        diffuse(nc, "d2", dram["tilesT"], T, mem, True)
        nodes_stage(nc, T, mem, x1_dram, dram["tiles"])
        attend(nc, T, mem, dram["tiles"], x1_dram, y)


def layouts(x, adj, L0_gnn_W, L1_gnn_W, L1_gnn_b, L1_gnn_a_s, L1_gnn_a_r):
    N = x.shape[0]
    T, S = N // P, N // SPAN
    c = np.ascontiguousarray
    return {
        "tilesT": c(adj.reshape(S, SPAN, T, P).transpose(0, 2, 3, 1)).reshape(S * T, P, SPAN),
        "tiles": c(adj.reshape(T, P, S, SPAN).transpose(0, 2, 1, 3)).reshape(T * S, P, SPAN),
        "xn": c(x.reshape(T, P, P).transpose(1, 0, 2)),
        "xT": c(x.T),
        "w_cheb": c(L0_gnn_W.transpose(2, 0, 1)),
        "w_att": c(L1_gnn_W.T),
        "w_att_rows": c(L1_gnn_W),
        "b_col": c(L1_gnn_b.reshape(P, 1)),
        "a_s": c(L1_gnn_a_s), "a_r": c(L1_gnn_a_r),
        "ident": np.eye(P, dtype=np.float32),
    }


def kernel(x, adj, L0_gnn_W, L1_gnn_W, L1_gnn_b, L1_gnn_a_s, L1_gnn_a_r):
    import concourse.bacc as bacc
    from concourse.bass_utils import run_bass_kernel_spmd

    args = [np.asarray(a) for a in (x, adj, L0_gnn_W, L1_gnn_W, L1_gnn_b, L1_gnn_a_s, L1_gnn_a_r)]
    arrays = layouts(*args)
    N = args[0].shape[0]
    nc = bacc.Bacc("TRN2", target_bir_lowering=False, num_devices=1)
    dram = {k: nc.dram_tensor(k, a.shape, mybir.dt.from_np(a.dtype), kind="ExternalInput").ap() for k, a in arrays.items()}
    y = nc.dram_tensor("y", (N // P, P, P), F32, kind="ExternalOutput").ap()
    build(nc, dram, y)
    r = run_bass_kernel_spmd(nc, [arrays], core_ids=[0])
    return r.results[0]["y"].reshape(N, P)
```
